# Optimizing a Trainium2 kernel written in Bass

```python
import numpy as np
import jax
import jax.numpy as jnp

def _softmax(x, axis=-1):
    return jax.nn.softmax(x, axis=axis)

def _gelu(x):
    return jax.nn.gelu(x, approximate=True)

def _silu(x):
    return jax.nn.silu(x)

def _sigmoid(x):
    return jax.nn.sigmoid(x)

def _layernorm(x, axis=-1, eps=1e-05):
    m = jnp.mean(x, axis=axis, keepdims=True)
    v = jnp.var(x, axis=axis, keepdims=True)
    return (x - m) / jnp.sqrt(v + eps)

def _scatter_add(tgt, idx, src, axis=0):
    return tgt.at[idx].add(src)

def _segment_sum(src, seg, n):
    return jax.ops.segment_sum(src, seg, n)
kernel_name = 'mk_lm_tower_d1_tok_ids512_r4_62af30'

def setup_inputs(seed: int=0):
    np.random.seed(seed)
    _w = jnp.asarray

    def _rec_inputs():
        import jax
        import jax.numpy as jnp
        _rk = jax.random.key(seed)
        x = jax.random.randint(jax.random.fold_in(_rk, 1), (8, 512), 0, 12564, jnp.int32)
        return x
    x = _rec_inputs()

    def _L0_tok_setup():
        import jax, jax.numpy as jnp
        import numpy as np
        VOCAB = 50257
        EMBED_DIM = 128
        PADDING_IDX = 0
        key = jax.random.key(seed)
        k1, k2 = jax.random.split(key)
        token_ids = jax.random.randint(k1, (8, 1024), 0, VOCAB, dtype=jnp.int64 if jax.config.jax_enable_x64 else jnp.int32)
        W = jax.random.normal(k2, (EMBED_DIM, VOCAB), dtype=jnp.float32) * (1.0 / np.sqrt(VOCAB))
        return {'token_ids': token_ids, 'W': W}
    _L0_tok_all = _L0_tok_setup()
    _L0_tok_in = {k: v for k, v in _L0_tok_all.items() if k in ('W',)}
    del _L0_tok_all

    def _L0_attn_setup():
        import math
        import jax, jax.numpy as jnp
        import numpy as np
        B, T, D, H = (2, 512, 128, 8)

        def layer_norm(x, g, b, eps=1e-05):
            mu = x.mean(-1, keepdims=True)
            var = ((x - mu) ** 2).mean(-1, keepdims=True)
            return (x - mu) / jnp.sqrt(var + eps) * g + b
        key = jax.random.key(seed)
        ks = jax.random.split(key, 6)
        s = 1.0 / math.sqrt(D)
        return {'x': jax.random.normal(ks[0], (B, T, D), dtype=jnp.float32), 'P': jax.random.normal(ks[1], (H, D, D), dtype=jnp.float32) * s, 'Q': jax.random.normal(ks[2], (H, D, D), dtype=jnp.float32) * s, 'gamma': jnp.ones((D,), jnp.float32), 'beta': jnp.zeros((D,), jnp.float32), 'W1': jax.random.normal(ks[3], (2 * D, D), dtype=jnp.float32) * s, 'b1': jnp.zeros((2 * D,), jnp.float32), 'W2': jax.random.normal(ks[4], (D, 2 * D), dtype=jnp.float32) * (1.0 / math.sqrt(2 * D)), 'b2': jnp.zeros((D,), jnp.float32), 'Wp': jax.random.normal(ks[5], (D, D), dtype=jnp.float32) * s, 'bp': jnp.zeros((D,), jnp.float32)}
    _L0_attn_all = _L0_attn_setup()
    _L0_attn_in = {k: v for k, v in _L0_attn_all.items() if k in ('P', 'Q', 'gamma', 'beta', 'W1', 'b1', 'W2', 'b2', 'Wp', 'bp')}
    del _L0_attn_all

    def _L0_ffn_setup():
        import jax, jax.numpy as jnp
        import numpy as np
        E = 64
        K = 2
        D = 128
        H = 64
        NSH = 2
        ROUTE_SCALE = 2.5
        CAP = 256
        STD = 0.02
        key = jax.random.key(seed)
        ks = jax.random.split(key, 8)
        x = jax.random.normal(ks[0], (4, 512, D), dtype=jnp.float32)
        gate_w = jax.random.normal(ks[1], (E, D), dtype=jnp.float32) * STD
        w1 = jax.random.normal(ks[2], (E, D, H), dtype=jnp.float32) * STD
        w3 = jax.random.normal(ks[3], (E, D, H), dtype=jnp.float32) * STD
        w2 = jax.random.normal(ks[4], (E, H, D), dtype=jnp.float32) * STD
        sw1 = jax.random.normal(ks[5], (D, H * NSH), dtype=jnp.float32) * STD
        sw3 = jax.random.normal(ks[6], (D, H * NSH), dtype=jnp.float32) * STD
        sw2 = jax.random.normal(ks[7], (H * NSH, D), dtype=jnp.float32) * STD
        return {'x': x, 'gate_w': gate_w, 'w1': w1, 'w3': w3, 'w2': w2, 'sw1': sw1, 'sw3': sw3, 'sw2': sw2}
    _L0_ffn_all = _L0_ffn_setup()
    _L0_ffn_in = {k: v for k, v in _L0_ffn_all.items() if k in ('gate_w', 'w1', 'w3', 'w2', 'sw1', 'sw3', 'sw2')}
    del _L0_ffn_all
    return {'x': x, 'L0_tok_W': _L0_tok_in['W'], 'L0_attn_P': _L0_attn_in['P'], 'L0_attn_Q': _L0_attn_in['Q'], 'L0_attn_gamma': _L0_attn_in['gamma'], 'L0_attn_beta': _L0_attn_in['beta'], 'L0_attn_W1': _L0_attn_in['W1'], 'L0_attn_b1': _L0_attn_in['b1'], 'L0_attn_W2': _L0_attn_in['W2'], 'L0_attn_b2': _L0_attn_in['b2'], 'L0_attn_Wp': _L0_attn_in['Wp'], 'L0_attn_bp': _L0_attn_in['bp'], 'L0_ffn_gate_w': _L0_ffn_in['gate_w'], 'L0_ffn_w1': _L0_ffn_in['w1'], 'L0_ffn_w3': _L0_ffn_in['w3'], 'L0_ffn_w2': _L0_ffn_in['w2'], 'L0_ffn_sw1': _L0_ffn_in['sw1'], 'L0_ffn_sw3': _L0_ffn_in['sw3'], 'L0_ffn_sw2': _L0_ffn_in['sw2']}

def reference(x, L0_tok_W, L0_attn_P, L0_attn_Q, L0_attn_gamma, L0_attn_beta, L0_attn_W1, L0_attn_b1, L0_attn_W2, L0_attn_b2, L0_attn_Wp, L0_attn_bp, L0_ffn_gate_w, L0_ffn_w1, L0_ffn_w3, L0_ffn_w2, L0_ffn_sw1, L0_ffn_sw3, L0_ffn_sw2):
    import jax
    import jax.numpy as jnp

    def _L0_tok_ref(token_ids, W):
        import jax, jax.numpy as jnp
        import numpy as np
        VOCAB = 50257
        EMBED_DIM = 128
        PADDING_IDX = 0
        emb = jnp.take(W.T, token_ids, axis=0)
        mask = (token_ids != PADDING_IDX)[..., None]
        return jnp.where(mask, emb, jnp.zeros((), emb.dtype))

    def _L0_attn_ref(x, P, Q, gamma, beta, W1, b1, W2, b2, Wp, bp):
        import math
        import jax, jax.numpy as jnp
        import numpy as np
        B, T, D, H = (2, 512, 128, 8)

        def layer_norm(x, g, b, eps=1e-05):
            mu = x.mean(-1, keepdims=True)
            var = ((x - mu) ** 2).mean(-1, keepdims=True)
            return (x - mu) / jnp.sqrt(var + eps) * g + b
        Bx, Tx, d = x.shape
        h = P.shape[0]
        QZ = jnp.einsum('btd,hed->bhte', x, Q)
        PZ = jnp.einsum('btd,hed->bhte', x, P)
        scores = jnp.einsum('bhte,bse->bhts', QZ, x) / math.sqrt(d)
        mask = jnp.tril(jnp.ones((Tx, Tx), x.dtype))
        scores = scores * mask
        y = jnp.einsum('bhts,bhse->bte', scores, PZ) / h
        z = layer_norm(y + x, gamma, beta)
        m = jnp.maximum(z @ W1.T + b1, 0.0) @ W2.T + b2
        z = z + m
        return z @ Wp.T + bp

    def _L0_ffn_ref(x, gate_w, w1, w3, w2, sw1, sw3, sw2):
        import jax, jax.numpy as jnp
        import numpy as np
        E = 64
        K = 2
        D = 128
        H = 64
        NSH = 2
        ROUTE_SCALE = 2.5
        CAP = 256
        STD = 0.02
        bs, slen, d = x.shape
        xf = x.reshape(-1, d)
        logits = xf @ gate_w.T
        scores = jax.nn.sigmoid(logits.astype(jnp.float32))
        top_scores, top_idx = jax.lax.top_k(scores, K)
        top_scores = top_scores / (top_scores.sum(-1, keepdims=True) + 1e-20)
        top_scores = top_scores * ROUTE_SCALE
        flat_e = top_idx.reshape(-1)
        x_pairs = jnp.repeat(xf, K, axis=0)
        oh = jax.nn.one_hot(flat_e, E, dtype=jnp.int32)
        pos = jnp.take_along_axis(jnp.cumsum(oh, axis=0), flat_e[:, None], axis=1)[:, 0] - 1
        buf = jnp.zeros((E, CAP, d), dtype=xf.dtype).at[flat_e, pos].set(x_pairs, mode='drop')
        h = jax.nn.silu(jnp.einsum('ecd,edh->ech', buf, w1)) * jnp.einsum('ecd,edh->ech', buf, w3)
        y = jnp.einsum('ech,ehd->ecd', h, w2)
        valid = (pos < CAP)[:, None]
        y_pairs = jnp.where(valid, y[flat_e, jnp.minimum(pos, CAP - 1)], 0.0)
        routed = (y_pairs.reshape(-1, K, d) * top_scores[..., None].astype(xf.dtype)).sum(axis=1)
        shared = jax.nn.silu(xf @ sw1) * (xf @ sw3) @ sw2
        return (shared + routed).reshape(bs, slen, d)
    h = _L0_tok_ref(x, L0_tok_W)
    h = h + _L0_attn_ref(_layernorm(h, axis=-1), L0_attn_P, L0_attn_Q, L0_attn_gamma, L0_attn_beta, L0_attn_W1, L0_attn_b1, L0_attn_W2, L0_attn_b2, L0_attn_Wp, L0_attn_bp)
    h = h + _L0_ffn_ref(_layernorm(h, axis=-1), L0_ffn_gate_w, L0_ffn_w1, L0_ffn_w3, L0_ffn_w2, L0_ffn_sw1, L0_ffn_sw3, L0_ffn_sw2)
    return h

_drawn_inputs = setup_inputs


def setup_inputs(seed=0):
    import zlib

    import numpy as np

    out = dict(_drawn_inputs(seed))
    spreads = {'L0_attn_gamma': (1.0, 0.2),
     'L0_attn_beta': (0.0, 0.1),
     'L0_attn_b1': (0.0, 0.1),
     'L0_attn_b2': (0.0, 0.1),
     'L0_attn_bp': (0.0, 0.1)}
    factors = {'L0_ffn_gate_w': 8.0,
     'L0_ffn_w1': 8.0,
     'L0_ffn_w3': 8.0,
     'L0_ffn_w2': 8.0,
     'L0_ffn_sw1': 8.0,
     'L0_ffn_sw3': 8.0,
     'L0_ffn_sw2': 8.0}
    for name, (base, spread) in spreads.items():
        noise = np.random.default_rng([zlib.crc32(name.encode()), seed]).standard_normal(out[name].shape)
        drawn = base * np.exp(spread * noise) if base else spread * noise
        out[name] = jnp.asarray(drawn.astype(out[name].dtype))
    for name, factor in factors.items():
        out[name] = (out[name] * factor).astype(out[name].dtype)
    return out
```

```python
from contextlib import ExitStack

import concourse.bass as bass
from concourse import mybir
from concourse.alu_op_type import AluOpType as ALU

ACT = mybir.ActivationFunctionType
AXES = mybir.AxisListType
F32 = mybir.dt.float32
F32R = mybir.dt.float32r
BF16 = mybir.dt.bfloat16
I32 = mybir.dt.int32
U32 = mybir.dt.uint32

P = 128

TOP_K = 2
CAP = 256
ROUTE_SCALE = 2.5
LN_EPS = 1e-5
PADDING_IDX = 0
DROPPED = 1 << 20

HEADS = 8
GROUPS = 8
FRONT = ["T1", "Q0", "Q1", "X", "Q2", "Q3", "Q4", "Q5", "Q6", "Q7", "SC0", "SC1"]
for _k in range(GROUPS - 2):
    FRONT += [f"SC{_k + 2}", f"U{_k}"]
FRONT += ["U6", "U7"]
BACK = ["Y", "T2", "T3", "W1a", "W1b", "W2", "WP", "T4", "G", "S1", "S3", "C", "SW2"]
NF = len(FRONT)
FRONT_BANKS = 5
BACK_BANKS = 3


def front_bank(name):
    return FRONT.index(name) % FRONT_BANKS


def front_before(name):
    at = FRONT.index(name)
    if at >= FRONT_BANKS:
        return at - FRONT_BANKS + 1
    last = max(k for k in range(NF) if k % FRONT_BANKS == at)
    return last + 1 - NF


def back_bank(name):
    return FRONT_BANKS + BACK.index(name) % BACK_BANKS


def back_before(name):
    at = BACK.index(name)
    if at >= BACK_BANKS:
        return BACK[at - BACK_BANKS], False
    last = max(k for k in range(len(BACK)) if k % BACK_BANKS == at)
    return BACK[last], True


def tower(nc, ids, embed, pT, qT, gamma, beta, w1T, b1, w2T, b2, wpT, bp, gateT, ew13, ew2, sw1, sw3, sw2, out):
    NB, S, D = out.shape
    C = S // P
    TILES = NB * C
    H = qT.shape[1]
    E = gateT.shape[1]
    EH = ew2.shape[1]
    PAIRS = E // 2
    SLOTS = E * CAP
    HG = H // 2
    SCORE_SCALE = 1.0 / (H * float(D) ** 0.5)
    assert D == P and C == 4 and H == HEADS and H * C // HG == GROUPS and CAP == 2 * P and EH == P // 2

    out_v = out.rearrange("b (c p) d -> b p c d", p=P)
    xbuf = nc.dram_tensor("expert_rows_in", (SLOTS, D), F32, kind="Internal").ap()
    ybuf = nc.dram_tensor("expert_rows_out", (SLOTS, D), F32, kind="Internal").ap()
    xbuf_v = xbuf.rearrange("(q e p r) d -> q p e (r d)", e=2, p=P, r=2)
    ybuf_v = ybuf.rearrange("(q e p r) d -> q p e (r d)", e=2, p=P, r=2)
    ZW = 1024
    xbuf_z = xbuf.rearrange("(z p r) d -> z p (r d)", p=P, r=ZW // D)
    NZ = SLOTS * D // (P * ZW)

    ctx = ExitStack()
    with ctx:
        def sb(name, shape, dt=F32):
            return ctx.enter_context(nc.sbuf_tensor(name, shape, dt))

        def sem(name):
            return ctx.enter_context(nc.semaphore(name))

        identity = sb("identity", [P, P])
        upper = sb("upper", [P, P], BF16)
        ones = sb("ones", [P, P], BF16)
        expert_iota = sb("expert_iota", [P, E])
        minus_half = sb("minus_half", [P, C])
        zeros = sb("zeros", [P, ZW])
        ids_sb = sb("ids_sb", [P, TILES], I32)
        not_pad = sb("not_pad", [P, TILES])
        raw_w = sb("raw_w", [P, H, D])
        q_hi, q_lo = sb("q_hi", [P, H, D], F32R), sb("q_lo", [P, H, D], F32R)
        p_hi, p_lo = sb("p_hi", [P, H, D], F32R), sb("p_lo", [P, H, D], F32R)
        gamma_sb, beta_sb, b2_sb = sb("gamma_sb", [P, 1]), sb("beta_sb", [P, 1]), sb("b2_sb", [P, 1])
        b1_sb = sb("b1_sb", [P, 2])
        bp_sb = sb("bp_sb", [P, D])
        w1_sb, w2_sb, wp_sb = sb("w1_sb", [P, 2 * D]), sb("w2_sb", [P, 2, D]), sb("wp_sb", [P, D])
        gate_sb = sb("gate_sb", [P, E])
        sw1_sb, sw3_sb, sw2_sb = sb("sw1_sb", [P, D]), sb("sw3_sb", [P, D]), sb("sw2_sb", [P, D])

        stream = sb("stream", [P, TILES, D])
        pair_slot = sb("pair_slot", [P, NB, TOP_K * C], I32)
        pair_weight = sb("pair_weight", [P, NB, TOP_K * C])

        ids_now = sb("ids_now", [P, C], I32)
        gathered = sb("gathered", [P, C, D])
        emb = sb("emb", [P, C, D])
        stats1, mv1 = sb("stats1", [P, C, 6]), sb("mv1", [P, C, 2])
        var1, rstd1 = sb("var1", [P, C]), sb("rstd1", [P, C])
        xn = sb("xn", [P, C, D])
        x_hi, x_lo = sb("x_hi", [P, C, D], F32R), sb("x_lo", [P, C, D], F32R)
        xt_hi, xt_lo = sb("xt_hi", [P, S], F32R), sb("xt_lo", [P, S], F32R)
        xt = sb("xt", [P, S])
        state = sb("state", [P, C - 1, D])
        st_hi, st_lo = sb("st_hi", [P, C - 1, D], F32R), sb("st_lo", [P, C - 1, D], F32R)
        qz_hi, qz_lo = sb("qz_hi", [P, H, S], F32R), sb("qz_lo", [P, H, S], F32R)
        sc_hi, sc_lo = sb("sc_hi", [P, 4, HG, P], F32R), sb("sc_lo", [P, 4, HG, P], F32R)
        ut_hi, ut_lo = sb("ut_hi", [P, H, S], F32R), sb("ut_lo", [P, H, S], F32R)
        vt = sb("vt", [P, S])
        stats2, mv2 = sb("stats2", [P, C, 6]), sb("mv2", [P, C, 2])
        var2, rstd2 = sb("var2", [P, C]), sb("rstd2", [P, C])
        z0 = sb("z0", [P, C, D])
        zt = sb("zt", [P, S])
        m1 = sb("m1", [P, 2, S])
        z2t = sb("z2t", [P, S])
        stats3, mv3 = sb("stats3", [P, C, 6]), sb("mv3", [P, C, 2])
        var3, rstd3 = sb("var3", [P, C]), sb("rstd3", [P, C])
        xf = sb("xf", [P, C, D])
        xft = sb("xft", [P, S])
        scores = sb("scores", [P, C, E])
        top8, index8 = sb("top8", [P, C, 8]), sb("index8", [P, C, 8], U32)
        index2 = sb("index2", [P, TOP_K, C])
        chosen = sb("chosen", [P, TOP_K, C, E])
        chosen_pos = sb("chosen_pos", [P, TOP_K, C, E])
        either = sb("either", [P, C, E], BF16)
        seen, seen_new = sb("seen", [P, E], BF16), sb("seen_new", [P, E])
        pos = sb("pos", [P, TOP_K, C])
        kept = sb("kept", [P, TOP_K, C])
        pos_in = sb("pos_in", [P, TOP_K, C])
        slot_f = sb("slot_f", [P, TOP_K, C])
        slot_drop = sb("slot_drop", [P, TOP_K, C])
        slot_out = sb("slot_out", [P, TOP_K * C], I32)
        top_sum, top_inv = sb("top_sum", [P, C]), sb("top_inv", [P, C])
        weight = sb("weight", [P, TOP_K, C])
        sig, gated, hs = sb("sig", [P, S]), sb("gated", [P, S]), sb("hs", [P, S])
        rows = [sb(f"rows{k}", [P, 2, 2 * D]) for k in range(2)]
        w13 = [sb(f"w13_{k}", [P, 2, P]) for k in range(2)]
        w2e = [sb(f"w2e_{k}", [P, 2, D]) for k in range(2)]
        rows_t = [m1[:, k, :].rearrange("p (m s) -> p m s", s=P) for k in range(2)]
        silu = [sig, gated]
        hidden = [hs, z2t]
        y_sb = [sb(f"y_sb{k}", [P, 2, 2 * D]) for k in range(2)]
        slot_now = [sb(f"slot_now{k}", [P, TOP_K * C], I32) for k in range(2)]
        y_got = [sb(f"y_got{k}", [P, TOP_K * C, D]) for k in range(2)]

        banks = [ctx.enter_context(nc.psum_tensor(f"bank{k}", [P, S], F32)) for k in range(8)]

        wait_carried = sem("wait_carried")
        w_q = sem("w_q_landed")
        w_p = sem("w_p_landed")
        w_small = sem("small_weights_landed")
        w_ids = sem("ids_landed")
        const_made = sem("constants_made")
        const_step = sem("constant_begun")
        start_split = sem("start_weights_split")
        q_split = sem("q_p_split")
        pad_made = sem("pad_mask_made")
        zero_made = sem("zeros_made")
        zero_filled = sem("expert_rows_zeroed")
        ids_copied = sem("ids_copied")
        emb_landed = sem("embeddings_landed")
        emb_masked = sem("embeddings_masked")
        stream_begun = sem("stream_begun")
        ln1_stats, ln1_mean, ln1_var = sem("ln1_stats"), sem("ln1_mean"), sem("ln1_var")
        ln1_rstd, xn_ready = sem("ln1_rstd"), sem("xn_ready")
        x_hi_ready, x_split = sem("x_hi_ready"), sem("x_split")
        front_full, front_hi, front_free = sem("front_full"), sem("front_hi"), sem("front_free")
        state_step, state_hi, state_split = sem("state_step"), sem("state_hi"), sem("state_split")
        masked = sem("scores_masked")
        full = {n: sem(f"{n}_full") for n in BACK}
        free = {n: sem(f"{n}_free") for n in BACK}
        ln2_stats, ln2_mean, ln2_var = sem("ln2_stats"), sem("ln2_mean"), sem("ln2_var")
        ln2_rstd = sem("ln2_rstd")
        ln3_stats, ln3_mean, ln3_var = sem("ln3_stats"), sem("ln3_mean"), sem("ln3_var")
        ln3_rstd, xf_ready = sem("ln3_rstd"), sem("xf_ready")
        top_found, index_found, index_float = sem("top_found"), sem("index_found"), sem("index_float")
        chosen_made, either_made = sem("chosen_made"), sem("either_made")
        seen_sum, seen_made = sem("seen_sum"), sem("seen_made")
        pos_made, kept_made, slot_made = sem("pos_made"), sem("kept_made"), sem("slot_made")
        slots_ready, rows_sent = sem("slots_ready"), sem("rows_sent")
        weight_step, weight_ready = sem("weight_step"), sem("weight_ready")
        sig_ready, gated_ready = sem("sig_ready"), sem("gated_ready")
        rows_landed = [sem(f"rows_landed{k}") for k in range(2)]
        rows_t_full, rows_t_ready = sem("rows_t_full"), sem("rows_t_ready")
        gu_full, silu_ready, hidden_ready = sem("gu_full"), sem("silu_ready"), sem("hidden_ready")
        y_full, y_ready = sem("y_full"), sem("y_ready")
        y_stored = [sem(f"y_stored{k}") for k in range(2)]
        slot_copied = sem("slot_copied")
        y_landed = [sem(f"y_landed{k}") for k in range(2)]
        pair_added, tiles_done = sem("pair_added"), sem("tiles_done")
        out_stored = sem("out_stored")

        SMALL = 12
        block = ctx.enter_context(nc.Block())

        def wait(eng, s, value):
            if not (isinstance(value, int) and value <= 0):
                eng.wait_ge(s, value)

        def carried(eng):
            eng.sem_inc(wait_carried, 1)

        def tile_slice(i):
            return bass.ds(i * C, C)

        @block.sync
        def _(sp):
            sp.dma_start(ids_sb[:], ids).then_inc(w_ids, 16)
            sp.dma_start(raw_w[:], qT).then_inc(w_q, 16)
            for dst, src in ((gamma_sb[:], gamma), (beta_sb[:], beta), (b1_sb[:], b1), (b2_sb[:], b2),
                             (bp_sb[:], bp.broadcast_to([P, D])),
                             (w1_sb[:], w1T), (w2_sb[:], w2T), (wp_sb[:], wpT), (gate_sb[:], gateT),
                             (sw1_sb[:], sw1), (sw3_sb[:], sw3), (sw2_sb[:], sw2)):
                sp.dma_start(dst, src).then_inc(w_small, 16)
            sp.wait_ge(start_split, 1)
            sp.dma_start(raw_w[:], pT).then_inc(w_p, 16)
            sp.wait_ge(zero_made, 1)
            with sp.Fori(0, NZ) as z:
                sp.dma_start(xbuf_z[bass.ds(z, 1)].rearrange("z p n -> p (z n)"), zeros[:]).then_inc(zero_filled, 16)

            def load_pair(q, k):
                sp.dma_start(w13[k][:], ew13[bass.ds(q, 1)].rearrange("q p e f -> p (q e) f")).then_inc(rows_landed[k], 16)
                sp.dma_start(w2e[k][EH:P], ew2[bass.ds(q, 1)].rearrange("q f e d -> f (q e) d")).then_inc(rows_landed[k], 16)
                sp.dma_start(rows[k][:], xbuf_v[bass.ds(q, 1)].rearrange("q p e n -> p (q e) n")).then_inc(rows_landed[k], 16)

            sp.wait_ge(rows_sent, 16 * TILES * TOP_K)
            for k in range(2):
                load_pair(k, k)
            with sp.Fori(1, PAIRS // 2) as g:
                for k in range(2):
                    sp.wait_ge(y_full, g * 2 + (k - 1))
                    load_pair(g * 2 + k, k)

            with sp.Fori(0, NB) as i:
                sp.wait_ge(tiles_done, i + 1)
                sp.dma_start(out_v[bass.ds(i, 1)].rearrange("b p c d -> p (b c) d"), stream[:, tile_slice(i), :]).then_inc(out_stored, 16)
            sp.wait_ge(out_stored, 16 * NB)

        @block.gpsimd
        def _(pool):
            pool.memset(zeros[:], 0.0).then_inc(zero_made, 1)
            pool.memset(identity[:], 0.0).then_inc(const_step, 1)
            pool.memset(upper[:], 1.0).then_inc(const_step, 1)
            pool.memset(ones[:], 1.0).then_inc(const_made, 1)
            pool.memset(minus_half[:], -0.5).then_inc(const_made, 1)
            pool.memset(seen[:], 0.0).then_inc(const_made, 1)
            pool.iota(expert_iota[:], pattern=[[1, E]], base=0, channel_multiplier=0,
                      allow_small_or_imprecise_dtypes=True).then_inc(const_made, 1)
            pool.wait_ge(const_step, 2)
            pool.affine_select(out=identity[:], in_=identity[:], compare_op=ALU.not_equal, fill=1.0,
                               base=0, pattern=[[-1, P]], channel_multiplier=1).then_inc(const_made, 1)
            pool.affine_select(out=upper[:], in_=upper[:], compare_op=ALU.is_gt, fill=0.0,
                               base=0, pattern=[[1, P]], channel_multiplier=-1).then_inc(const_made, 1)

            def gather(i):
                wait(pool, emb_landed, 16 * C * i if isinstance(i, int) else i * (16 * C))
                pool.tensor_copy(ids_now[:], ids_sb[:, tile_slice(i)]).then_inc(ids_copied, 1)
                pool.wait_ge(ids_copied, i + 1)
                wait(pool, emb_masked, i)
                carried(pool)
                for c in range(C):
                    pool.indirect_dma_start(
                        out=gathered[:, c, :], out_offset=None, in_=embed,
                        in_offset=bass.IndirectOffsetOnAxis(ap=ids_now[:, c:c + 1], axis=0)).then_inc(emb_landed, 16)

            def begin_stream(i):
                pool.wait_ge(ln1_var, i + 1)
                pool.tensor_tensor(rstd1[:], var1[:], minus_half[:], ALU.pow).then_inc(ln1_rstd, 1)
                pool.tensor_tensor(stream[:, tile_slice(i), :], emb[:],
                                   bp_sb[:].unsqueeze(1).broadcast_to([P, C, D]), ALU.add).then_inc(stream_begun, 1)

            def state_low(i):
                pool.wait_ge(state_hi, i + 1)
                pool.tensor_tensor(st_lo[:], state[:], st_hi[:].bitcast(F32), ALU.subtract).then_inc(state_split, 1)

            def mask(i, k):
                pool.wait_ge(front_free, i * NF + FRONT.index(f"SC{k}") + 1)
                carried(pool)
                pool.affine_select(out=sc_hi[:, k % 4], in_=sc_hi[:, k % 4].bitcast(F32), compare_op=ALU.is_ge,
                                   fill=0.0, base=0, pattern=[[0, HG], [1, P]], channel_multiplier=-1)
                pool.affine_select(out=sc_lo[:, k % 4], in_=sc_lo[:, k % 4].bitcast(F32), compare_op=ALU.is_ge,
                                   fill=0.0, base=0, pattern=[[0, HG], [1, P]], channel_multiplier=-1).then_inc(masked, 1)

            def rstd_mid(n):
                pool.wait_ge(ln2_var, n)
                pool.tensor_tensor(rstd2[:], var2[:], minus_half[:], ALU.pow).then_inc(ln2_rstd, 1)

            def rstd_last(n):
                pool.wait_ge(ln3_var, n)
                pool.tensor_tensor(rstd3[:], var3[:], minus_half[:], ALU.pow).then_inc(ln3_rstd, 1)

            def dispatch(n):
                pool.wait_ge(slots_ready, n)
                carried(pool)
                for m in range(TOP_K * C):
                    pool.indirect_dma_start(
                        out=xbuf, out_offset=bass.IndirectOffsetOnAxis(ap=slot_out[:, m:m + 1], axis=0),
                        in_=xf[:, m % C, :], in_offset=None,
                        bounds_check=SLOTS - 1, oob_is_err=False).then_inc(rows_sent, 16)

            def batch(i, more, behind):
                if more:
                    gather(i + 1)
                if behind:
                    rstd_mid(i)
                state_low(i)
                for k in range(GROUPS):
                    mask(i, k)
                    if k == 1 and more:
                        begin_stream(i + 1)
                    if k == 4 and behind:
                        rstd_last(i)
                if behind:
                    dispatch(i)

            pool.wait_ge(w_ids, 16)
            pool.wait_ge(w_small, 16 * SMALL)
            pool.wait_ge(const_made, 6)
            gather(0)
            begin_stream(0)
            batch(0, True, False)
            pool.wait_ge(zero_filled, 16 * NZ)
            with pool.Fori(1, NB - 1) as i:
                batch(i, True, True)
            batch(NB - 1, False, True)
            rstd_mid(NB)
            rstd_last(NB)
            dispatch(NB)

            def fetch(i, k):
                wait(pool, tiles_done, i - 1)
                pool.tensor_copy(slot_now[k][:], pair_slot[:, bass.ds(i, 1), :].rearrange("p b m -> p (b m)")).then_inc(slot_copied, 1)
                pool.wait_ge(slot_copied, i + 1)
                carried(pool)
                for m in range(TOP_K * C):
                    pool.indirect_dma_start(
                        out=y_got[k][:, m, :], out_offset=None, in_=ybuf,
                        in_offset=bass.IndirectOffsetOnAxis(ap=slot_now[k][:, m:m + 1], axis=0)).then_inc(y_landed[k], 16)

            for k in range(2):
                pool.wait_ge(y_stored[k], 16 * PAIRS // 2)
            pool.wait_ge(weight_ready, NB)
            fetch(0, 0)
            fetch(1, 1)
            with pool.Fori(1, NB // 2) as g:
                for k in range(2):
                    fetch(g * 2 + k, k)

        @block.scalar
        def _(act):
            act.wait_ge(w_q, 16)
            act.copy(q_hi[:], raw_w[:]).then_inc(q_split, 1)
            act.wait_ge(w_p, 16)
            act.copy(p_hi[:], raw_w[:]).then_inc(q_split, 1)

            def leading(i, name, dst, scale=1.0):
                b = banks[front_bank(name)]
                act.wait_ge(front_full, i * NF + FRONT.index(name) + 1)
                src = b[:] if len(dst.shape) == 2 else b[:].rearrange("p (a b) -> p a b", b=P)
                act.activation(dst, src, ACT.Copy, scale=scale).then_inc(front_hi, 1)

            def gamma_beta(n):
                act.wait_ge(full["T3"], n)
                act.activation(zt[:], banks[back_bank("T3")][:], ACT.Identity, bias=beta_sb[:], scale=gamma_sb[:]).then_inc(free["T3"], 1)

            def relu(n, j):
                name = "W1a" if j == 0 else "W1b"
                act.wait_ge(full[name], n)
                act.activation(m1[:, j, :], banks[back_bank(name)][:], ACT.Relu, bias=b1_sb[:, j:j + 1]).then_inc(free[name], 1)

            def copy_xft(n):
                act.wait_ge(full["T4"], n)
                act.activation(xft[:], banks[back_bank("T4")][:], ACT.Copy).then_inc(free["T4"], 1)

            def gate_sigmoid(n):
                act.wait_ge(full["G"], n)
                act.activation(scores[:], banks[back_bank("G")][:, 0:C * E].rearrange("p (c e) -> p c e", e=E),
                               ACT.Sigmoid).then_inc(free["G"], 1)

            def shared_sigmoid(n):
                act.wait_ge(full["S1"], n)
                act.activation(sig[:], banks[back_bank("S1")][:], ACT.Sigmoid).then_inc(sig_ready, 1)

            def batch(i, behind):
                leading(i, "T1", xt_hi[:])
                leading(i, "Q0", qz_hi[:, 0, :], SCORE_SCALE)
                leading(i, "Q1", qz_hi[:, 1, :], SCORE_SCALE)
                act.wait_ge(state_step, 3 * i + 3 if isinstance(i, int) else i * 3 + 3)
                act.copy(st_hi[:], state[:]).then_inc(state_hi, 1)
                for h in range(2, H):
                    leading(i, f"Q{h}", qz_hi[:, h, :], SCORE_SCALE)
                if behind:
                    gamma_beta(i)
                for name in FRONT[FRONT.index("SC0"):]:
                    k = int(name[-1])
                    if name.startswith("SC"):
                        leading(i, name, sc_hi[:, k % 4])
                    else:
                        c, g = k // 2, k % 2
                        leading(i, name, ut_hi[:, HG * g:HG * g + HG, c * P:(c + 1) * P])
                    if behind:
                        if name == "SC1":
                            relu(i, 0)
                            relu(i, 1)
                        if name == "SC7":
                            copy_xft(i)
                if behind:
                    gate_sigmoid(i)
                    shared_sigmoid(i)

            batch(0, False)
            with act.Fori(1, NB) as i:
                batch(i, True)
            gamma_beta(NB)
            relu(NB, 0)
            relu(NB, 1)
            copy_xft(NB)
            gate_sigmoid(NB)
            shared_sigmoid(NB)

            def expert_pair(q, k):
                act.wait_ge(gu_full, q + 1)
                act.activation(silu[k][EH:P, :], banks[2 + k][0:EH, :], ACT.Silu).then_inc(silu_ready, 1)
                act.wait_ge(y_full, q + 1)
                wait(act, y_stored[k], (q // 2) * 16)
                act.activation(y_sb[k][:].rearrange("p e n -> p (e n)"), banks[4 + k][:], ACT.Copy).then_inc(y_ready, 1)
                act.wait_ge(y_ready, q + 1)
                act.dma_start(ybuf_v[bass.ds(q, 1)].rearrange("q p e n -> p (q e) n"), y_sb[k][:]).then_inc(y_stored[k], 16)

            def expert_pair_at(g, k):
                q = g * 2 + k
                act.wait_ge(gu_full, q + 1)
                act.activation(silu[k][EH:P, :], banks[2 + k][0:EH, :], ACT.Silu).then_inc(silu_ready, 1)
                act.wait_ge(y_full, q + 1)
                act.wait_ge(y_stored[k], g * 16)
                act.activation(y_sb[k][:].rearrange("p e n -> p (e n)"), banks[4 + k][:], ACT.Copy).then_inc(y_ready, 1)
                act.wait_ge(y_ready, q + 1)
                act.dma_start(ybuf_v[bass.ds(q, 1)].rearrange("q p e n -> p (q e) n"), y_sb[k][:]).then_inc(y_stored[k], 16)

            for k in range(2):
                expert_pair(k, k)
            with act.Fori(1, PAIRS // 2) as g:
                for k in range(2):
                    expert_pair_at(g, k)

        @block.vector
        def _(dve):
            dve.wait_ge(w_ids, 16)
            dve.tensor_scalar(not_pad[:], ids_sb[:], float(PADDING_IDX), None, ALU.not_equal).then_inc(pad_made, 1)
            dve.wait_ge(q_split, 1)
            dve.tensor_tensor(q_lo[:], raw_w[:], q_hi[:].bitcast(F32), ALU.subtract).then_inc(start_split, 1)
            for name in BACK:
                if name in [back_before(x)[0] for x in BACK if back_before(x)[1]]:
                    dve.sem_inc(free[name], 1)

            dve.sem_inc(seen_made, 1)

            def mean_var(stats, mv, var, source, s_stats, s_mean, s_var, n):
                carried(dve)
                for c in range(C):
                    dve.bn_stats(stats[:, c, :], source[:, c, :]).then_inc(s_stats, 1)
                dve.wait_ge(s_stats, n * C)
                carried(dve)
                for c in range(C):
                    dve.bn_aggr(mv[:, c, :], stats[:, c, :]).then_inc(s_mean, 1)
                dve.wait_ge(s_mean, n * C)
                dve.tensor_scalar(var[:], mv[:, :, 1], LN_EPS, None, ALU.add).then_inc(s_var, 1)

            def embed_in(i):
                dve.wait_ge(emb_landed, i * (16 * C) + 16 * C)
                dve.wait_ge(pad_made, 1)
                wait(dve, stream_begun, i)
                dve.tensor_tensor(emb[:], gathered[:],
                                  not_pad[:, tile_slice(i)].unsqueeze(2).broadcast_to([P, C, D]),
                                  ALU.mult).then_inc(emb_masked, 1)
                dve.wait_ge(emb_masked, i + 1)
                mean_var(stats1, mv1, var1, emb, ln1_stats, ln1_mean, ln1_var, i + 1)

            def normalise(i):
                dve.wait_ge(ln1_rstd, i + 1)
                for c in range(C):
                    dve.tensor_scalar(xn[:, c, :], emb[:, c, :], mv1[:, c, 0:1], rstd1[:, c:c + 1],
                                      ALU.subtract, ALU.mult).then_inc(xn_ready, 1)

            def split_x(i):
                dve.wait_ge(xn_ready, i * C + C)
                dve.tensor_copy(x_hi[:], xn[:]).then_inc(x_hi_ready, 1)
                dve.wait_ge(x_hi_ready, i + 1)
                dve.tensor_tensor(x_lo[:], xn[:], x_hi[:].bitcast(F32), ALU.subtract).then_inc(x_split, 1)

            def rest(i, name, hi, lo, scale=1.0, last=True):
                b = banks[front_bank(name)]
                at = FRONT.index(name)
                dve.wait_ge(front_hi, i * (NF - 1) + (at + 1 if at < FRONT.index("X") else at))
                src = b[:] if len(hi.shape) == 2 else b[:].rearrange("p (a b) -> p a b", b=P)
                op = dve.scalar_tensor_tensor(lo, src, scale, hi.bitcast(F32), ALU.mult, ALU.subtract)
                if last:
                    op.then_inc(front_free, 1)

            def states(i):
                b = banks[front_bank("X")]
                dve.wait_ge(front_full, i * NF + FRONT.index("X") + 1)
                wait(dve, state_split, i)
                dve.tensor_copy(state[:, 0, :], b[:, 0:D]).then_inc(state_step, 1)
                dve.wait_ge(state_step, i * 3 + 1)
                dve.tensor_tensor(state[:, 1, :], state[:, 0, :], b[:, D:2 * D], ALU.add).then_inc(state_step, 1)
                dve.wait_ge(state_step, i * 3 + 2)
                dve.tensor_tensor(state[:, 2, :], state[:, 1, :], b[:, 2 * D:3 * D], ALU.add).then_inc(state_step, 1)
                dve.wait_ge(state_step, i * 3 + 3)
                dve.sem_inc(front_free, 1)

            def residual(n):
                dve.wait_ge(full["Y"], n)
                dve.tensor_tensor(vt[:], banks[back_bank("Y")][:], xt[:], ALU.add).then_inc(free["Y"], 1)

            def ln_mid(n):
                dve.wait_ge(full["T2"], n)
                v = banks[back_bank("T2")][:].rearrange("p (c d) -> p c d", d=D)
                mean_var(stats2, mv2, var2, v, ln2_stats, ln2_mean, ln2_var, n)

            def ln_mid_apply(n):
                v = banks[back_bank("T2")][:].rearrange("p (c d) -> p c d", d=D)
                dve.wait_ge(ln2_rstd, n)
                for c in range(C):
                    op = dve.tensor_scalar(z0[:, c, :], v[:, c, :], mv2[:, c, 0:1], rstd2[:, c:c + 1],
                                           ALU.subtract, ALU.mult)
                op.then_inc(free["T2"], 1)

            def mlp_out(n):
                dve.wait_ge(full["W2"], n)
                dve.scalar_tensor_tensor(z2t[:], banks[back_bank("W2")][:], b2_sb[:], zt[:], ALU.add, ALU.add).then_inc(free["W2"], 1)

            def attn_out(n, i):
                dve.wait_ge(full["WP"], n)
                dve.wait_ge(stream_begun, n)
                h = stream[:, tile_slice(i), :]
                dve.tensor_tensor(h, banks[back_bank("WP")][:].rearrange("p (c d) -> p c d", d=D), h, ALU.add).then_inc(free["WP"], 1)

            def ln_last(n, i):
                dve.wait_ge(free["WP"], n)
                carried(dve)
                for c in range(C):
                    dve.bn_stats(stats3[:, c, :], stream[:, bass.ds(i * C + c, 1), :].rearrange("p a d -> p (a d)")).then_inc(ln3_stats, 1)
                dve.wait_ge(ln3_stats, n * C)
                carried(dve)
                for c in range(C):
                    dve.bn_aggr(mv3[:, c, :], stats3[:, c, :]).then_inc(ln3_mean, 1)
                dve.wait_ge(ln3_mean, n * C)
                dve.tensor_scalar(var3[:], mv3[:, :, 1], LN_EPS, None, ALU.add).then_inc(ln3_var, 1)

            def ln_last_apply(n, i):
                dve.wait_ge(ln3_rstd, n)
                wait(dve, rows_sent, (n - 1) * (16 * TOP_K * C))
                for c in range(C):
                    op = dve.tensor_scalar(xf[:, c, :], stream[:, bass.ds(i * C + c, 1), :].rearrange("p a d -> p (a d)"),
                                           mv3[:, c, 0:1], rstd3[:, c:c + 1], ALU.subtract, ALU.mult)
                op.then_inc(xf_ready, 1)

            def choose(n):
                dve.wait_ge(free["G"], n)
                carried(dve)
                for c in range(C):
                    dve.max(top8[:, c, :], scores[:, c, :]).then_inc(top_found, 1)
                dve.wait_ge(top_found, n * C)
                carried(dve)
                for c in range(C):
                    dve.max_index(index8[:, c, :], top8[:, c, :], scores[:, c, :]).then_inc(index_found, 1)
                dve.wait_ge(index_found, n * C)
                dve.tensor_copy(index2[:], index8[:, :, 0:TOP_K].rearrange("p c k -> p k c")).then_inc(index_float, 1)
                dve.wait_ge(index_float, n)
                dve.tensor_tensor(chosen[:], index2[:].unsqueeze(3).broadcast_to([P, TOP_K, C, E]),
                                  expert_iota[:].unsqueeze(1).unsqueeze(1).broadcast_to([P, TOP_K, C, E]),
                                  ALU.is_equal).then_inc(chosen_made, 1)
                dve.wait_ge(chosen_made, n)
                dve.tensor_tensor(either[:], chosen[:, 0], chosen[:, 1], ALU.add).then_inc(either_made, 1)
                dve.wait_ge(either_made, n)

            def route(n, i):
                dve.wait_ge(full["C"], n)
                before = banks[back_bank("C")][:, 0:C * E].rearrange("p (c e) -> p c e", e=E)
                for k in range(TOP_K):
                    op = dve.tensor_tensor(chosen_pos[:, k], before, chosen[:, k], ALU.mult)
                    op.then_inc(pos_made, 1)
                dve.sem_inc(free["C"], 1)
                dve.tensor_reduce(seen_new[:], either[:].rearrange("p c e -> p e c"), AXES.X, ALU.add).then_inc(seen_sum, 1)
                dve.wait_ge(pos_made, n * 3 - 1)
                dve.tensor_reduce(pos[:], chosen_pos[:], AXES.X, ALU.add).then_inc(pos_made, 1)
                dve.wait_ge(seen_sum, n)
                dve.tensor_tensor(seen[:], seen[:], seen_new[:], ALU.add).then_inc(seen_made, 1)
                dve.wait_ge(pos_made, n * 3)
                dve.tensor_scalar(kept[:], pos[:], float(CAP), None, ALU.is_lt).then_inc(kept_made, 1)
                dve.tensor_scalar(pos_in[:], pos[:], float(CAP - 1), None, ALU.min).then_inc(kept_made, 1)
                dve.wait_ge(kept_made, n * 2)
                dve.scalar_tensor_tensor(slot_f[:], index2[:], float(CAP), pos_in[:], ALU.mult, ALU.add).then_inc(slot_made, 1)
                dve.tensor_scalar(slot_drop[:], kept[:], -float(DROPPED), float(DROPPED), ALU.mult, ALU.add).then_inc(slot_made, 1)
                dve.wait_ge(slot_made, n * 2)
                dve.tensor_tensor(slot_out[:].rearrange("p (k c) -> p k c", c=C), slot_f[:], slot_drop[:], ALU.add).then_inc(slots_ready, 1)
                dve.tensor_copy(pair_slot[:, bass.ds(i, 1), :].rearrange("p b (k c) -> p (b k) c", c=C), slot_f[:])
                tops = top8[:, :, 0:TOP_K].rearrange("p c k -> p k c")
                dve.tensor_tensor(top_sum[:], tops[:, 0], tops[:, 1], ALU.add).then_inc(weight_step, 1)
                dve.wait_ge(weight_step, n * 4 - 3)
                dve.tensor_scalar(top_sum[:], top_sum[:], 1e-20, None, ALU.add).then_inc(weight_step, 1)
                dve.wait_ge(weight_step, n * 4 - 2)
                dve.reciprocal(top_inv[:], top_sum[:]).then_inc(weight_step, 1)
                dve.wait_ge(weight_step, n * 4 - 1)
                dve.tensor_tensor(weight[:], tops, top_inv[:].unsqueeze(1).broadcast_to([P, TOP_K, C]), ALU.mult).then_inc(weight_step, 1)
                dve.wait_ge(weight_step, n * 4)
                dve.scalar_tensor_tensor(pair_weight[:, bass.ds(i, 1), :].rearrange("p b (k c) -> p (b k) c", c=C),
                                         weight[:], ROUTE_SCALE, kept[:], ALU.mult, ALU.mult).then_inc(weight_ready, 1)

            def shared_gate(n):
                dve.wait_ge(sig_ready, n)
                dve.tensor_tensor(gated[:], banks[back_bank("S1")][:], sig[:], ALU.mult).then_inc(free["S1"], 1)
                dve.wait_ge(free["S1"], n)
                dve.wait_ge(full["S3"], n)
                dve.tensor_tensor(hs[:], banks[back_bank("S3")][:], gated[:], ALU.mult).then_inc(free["S3"], 1)

            def shared_add(n, i):
                dve.wait_ge(full["SW2"], n)
                h = stream[:, tile_slice(i), :]
                dve.tensor_tensor(h, banks[back_bank("SW2")][:].rearrange("p (c d) -> p c d", d=D), h, ALU.add).then_inc(free["SW2"], 1)

            def batch(i, more, behind):
                split_x(i)
                rest(i, "T1", xt_hi[:], xt_lo[:], last=False)
                if behind:
                    residual(i)
                    dve.wait_ge(free["Y"], i)
                dve.tensor_copy(xt[:], banks[front_bank("T1")][:]).then_inc(front_free, 1)
                rest(i, "Q0", qz_hi[:, 0, :], qz_lo[:, 0, :], SCORE_SCALE)
                rest(i, "Q1", qz_hi[:, 1, :], qz_lo[:, 1, :], SCORE_SCALE)
                states(i)
                if behind:
                    ln_mid(i)
                for h in range(2, H):
                    rest(i, f"Q{h}", qz_hi[:, h, :], qz_lo[:, h, :], SCORE_SCALE)
                    if h == 4 and behind:
                        ln_mid_apply(i)
                for name in FRONT[FRONT.index("SC0"):]:
                    k = int(name[-1])
                    if name.startswith("SC"):
                        rest(i, name, sc_hi[:, k % 4], sc_lo[:, k % 4])
                    else:
                        c, g = k // 2, k % 2
                        at = (slice(None), slice(HG * g, HG * g + HG), slice(c * P, (c + 1) * P))
                        rest(i, name, ut_hi[at], ut_lo[at])
                    if name == "SC1" and more:
                        embed_in(i + 1)
                    if name == "U1" and more:
                        normalise(i + 1)
                    if behind:
                        if name == "U0":
                            mlp_out(i)
                        if name == "U1":
                            attn_out(i, i - 1)
                        if name == "SC4":
                            ln_last(i, i - 1)
                        if name == "SC6":
                            ln_last_apply(i, i - 1)
                if behind:
                    choose(i)
                    shared_gate(i)
                    route(i, i - 1)
                    shared_add(i, i - 1)

            embed_in(0)
            normalise(0)
            dve.wait_ge(q_split, 2)
            dve.tensor_tensor(p_lo[:], raw_w[:], p_hi[:].bitcast(F32), ALU.subtract).then_inc(start_split, 1)
            dve.wait_ge(w_small, 16 * SMALL)
            dve.wait_ge(const_made, 6)
            batch(0, True, False)
            with dve.Fori(1, NB - 1) as i:
                batch(i, True, True)
            batch(NB - 1, False, True)
            residual(NB)
            ln_mid(NB)
            ln_mid_apply(NB)
            mlp_out(NB)
            attn_out(NB, NB - 1)
            ln_last(NB, NB - 1)
            ln_last_apply(NB, NB - 1)
            choose(NB)
            shared_gate(NB)
            route(NB, NB - 1)
            shared_add(NB, NB - 1)

            def expert_pair(q, k):
                dve.wait_ge(rows_t_full, q + 1)
                dve.tensor_copy(rows_t[k][:], banks[k][:].rearrange("p (m s) -> p m s", s=P)).then_inc(rows_t_ready, 1)
                dve.wait_ge(silu_ready, q + 1)
                dve.tensor_tensor(hidden[k][EH:P, :], banks[2 + k][EH:P, :], silu[k][EH:P, :], ALU.mult).then_inc(hidden_ready, 1)

            with dve.Fori(0, PAIRS // 2) as g:
                for k in range(2):
                    expert_pair(g * 2 + k, k)

            def add_pairs(i, k, landed):
                dve.wait_ge(y_landed[k], landed)
                for m in range(TOP_K * C):
                    if m == C:
                        dve.wait_ge(pair_added, i * C + C)
                    h = stream[:, bass.ds(i * C + m % C, 1), :].rearrange("p a d -> p (a d)")
                    w = pair_weight[:, bass.ds(i, 1), m:m + 1].rearrange("p a m -> p (a m)")
                    op = dve.scalar_tensor_tensor(h, y_got[k][:, m, :], w, h, ALU.mult, ALU.add)
                    if m < C:
                        op.then_inc(pair_added, 1)
                op.then_inc(tiles_done, 1)

            dve.wait_ge(weight_ready, NB)
            with dve.Fori(0, NB // 2) as g:
                for k in range(2):
                    add_pairs(g * 2 + k, k, g * (16 * TOP_K * C) + 16 * TOP_K * C)

        @block.tensor
        def _(pe):
            def product(out_ap, pairs, start=True, stop=True):
                last = None
                for n, (ah, al, bh, bl) in enumerate(pairs):
                    pe.matmul(out_ap, ah, bh, start=start and n == 0, stop=False)
                    pe.matmul(out_ap, ah, bl, start=False, stop=False)
                    last = pe.matmul(out_ap, al, bh, start=False, stop=stop and n == len(pairs) - 1)
                return last

            def front_slot(i, name):
                value = i * NF + front_before(name)
                wait(pe, front_free, value)
                return banks[front_bank(name)]

            def back_slot(n, name):
                before, _ = back_before(name)
                pe.wait_ge(free[before], n)
                return banks[back_bank(name)]

            def transposes(dst, src):
                for c in range(C):
                    op = pe.transpose(dst[:, c * P:(c + 1) * P], src(c), identity[:])
                return op

            def t1(i):
                b = front_slot(i, "T1")
                pe.wait_ge(xn_ready, i * C + C)
                transposes(b, lambda c: xn[:, c, :]).then_inc(front_full, 1)

            def qz(i, h):
                b = front_slot(i, f"Q{h}")
                product(b[:], [(q_hi[:, h, :], q_lo[:, h, :], xt_hi[:], xt_lo[:])]).then_inc(front_full, 1)

            def outer(i):
                b = front_slot(i, "X")
                pe.wait_ge(x_split, i + 1)
                for c in range(C - 1):
                    op = product(b[:, c * D:(c + 1) * D], [(x_hi[:, c, :], x_lo[:, c, :], x_hi[:, c, :], x_lo[:, c, :])])
                op.then_inc(front_full, 1)

            def score(i, k):
                c, g = k // 2, k % 2
                b = front_slot(i, f"SC{k}")
                at = (slice(None), slice(HG * g, HG * g + HG), slice(c * P, (c + 1) * P))
                xs = slice(c * P, (c + 1) * P)
                product(b[:].rearrange("p (a b) -> p a b", b=P),
                        [(xt_hi[:, xs], xt_lo[:, xs], qz_hi[at], qz_lo[at])]).then_inc(front_full, 1)

            def weighted(i, k):
                c, g = k // 2, k % 2
                b = front_slot(i, f"U{k}")
                at = (slice(None), slice(HG * g, HG * g + HG), slice(c * P, (c + 1) * P))
                pe.wait_ge(masked, i * GROUPS + k + 1)
                pairs = [(x_hi[:, c, :], x_lo[:, c, :], sc_hi[:, k % 4], sc_lo[:, k % 4])]
                if c:
                    if k == 2:
                        pe.wait_ge(state_split, i + 1)
                    pairs.append((st_hi[:, c - 1, :], st_lo[:, c - 1, :], qz_hi[at], qz_lo[at]))
                product(b[:].rearrange("p (a b) -> p a b", b=P), pairs).then_inc(front_full, 1)

            def y_product(n):
                b = back_slot(n, "Y")
                pe.wait_ge(front_free, n * NF)
                product(b[:], [(p_hi[:, h, :], p_lo[:, h, :], ut_hi[:, h, :], ut_lo[:, h, :]) for h in range(H)]).then_inc(full["Y"], 1)

            def t2(n):
                b = back_slot(n, "T2")
                pe.wait_ge(free["Y"], n)
                transposes(b, lambda c: vt[:, c * P:(c + 1) * P]).then_inc(full["T2"], 1)

            def t3(n):
                b = back_slot(n, "T3")
                pe.wait_ge(free["T2"], n)
                transposes(b, lambda c: z0[:, c, :]).then_inc(full["T3"], 1)

            def mlp_in(n):
                pe.wait_ge(free["T3"], n)
                for j, name in enumerate(("W1a", "W1b")):
                    b = back_slot(n, name)
                    pe.matmul(b[:], w1_sb[:, j * P:(j + 1) * P], zt[:], start=True, stop=True).then_inc(full[name], 1)

            def mlp_down(n):
                b = back_slot(n, "W2")
                pe.wait_ge(free["W1b"], n)
                pe.matmul(b[:], w2_sb[:, 0, :], m1[:, 0, :], start=True, stop=False)
                pe.matmul(b[:], w2_sb[:, 1, :], m1[:, 1, :], start=False, stop=True).then_inc(full["W2"], 1)

            def project(n):
                b = back_slot(n, "WP")
                pe.wait_ge(free["W2"], n)
                for c in range(C):
                    op = pe.matmul(b[:, c * D:(c + 1) * D], z2t[:, c * P:(c + 1) * P], wp_sb[:], start=True, stop=True)
                op.then_inc(full["WP"], 1)

            def t4(n):
                b = back_slot(n, "T4")
                pe.wait_ge(xf_ready, n)
                transposes(b, lambda c: xf[:, c, :]).then_inc(full["T4"], 1)

            def gate(n):
                b = back_slot(n, "G")
                pe.wait_ge(free["T4"], n)
                for c in range(C):
                    op = pe.matmul(b[:, c * E:(c + 1) * E], xft[:, c * P:(c + 1) * P], gate_sb[:], start=True, stop=True)
                op.then_inc(full["G"], 1)

            def shared_in(n):
                for name, w in (("S1", sw1_sb), ("S3", sw3_sb)):
                    b = back_slot(n, name)
                    pe.matmul(b[:], w[:], xft[:], start=True, stop=True).then_inc(full[name], 1)

            def counts(n):
                b = back_slot(n, "C")
                pe.wait_ge(either_made, n)
                pe.wait_ge(seen_made, n)
                pe.matmul(b[:, 0:C * E], upper[:], either[:], start=True, stop=False)
                for c in range(C):
                    for before in range(c):
                        pe.matmul(b[:, c * E:(c + 1) * E], ones[:], either[:, before, :], start=False, stop=False)
                op = pe.matmul(b[:, 0:C * E], ones[:], seen[:].unsqueeze(1).broadcast_to([P, C, E]), start=False, stop=True)
                op.then_inc(full["C"], 1)

            def shared_out(n):
                b = back_slot(n, "SW2")
                pe.wait_ge(free["S3"], n + 1)
                for c in range(C):
                    op = pe.matmul(b[:, c * D:(c + 1) * D], hs[:, c * P:(c + 1) * P], sw2_sb[:], start=True, stop=True)
                op.then_inc(full["SW2"], 1)

            def batch(i, behind):
                t1(i)
                if behind:
                    y_product(i)
                pe.wait_ge(front_free, i * NF + 1)
                qz(i, 0)
                qz(i, 1)
                outer(i)
                for h in range(2, H):
                    if h == 4 and behind:
                        t2(i)
                    qz(i, h)
                score_after = FRONT.index("Q7") + 1
                if behind:
                    t3(i)
                pe.wait_ge(front_free, i * NF + score_after)
                score(i, 0)
                score(i, 1)
                if behind:
                    mlp_in(i)
                for k in range(2, GROUPS):
                    score(i, k)
                    weighted(i, k - 2)
                    if behind:
                        if k == 2:
                            mlp_down(i)
                        if k == 3:
                            project(i)
                        if k == 7:
                            t4(i)
                weighted(i, GROUPS - 2)
                if behind:
                    gate(i)
                    shared_in(i)
                weighted(i, GROUPS - 1)
                if behind:
                    counts(i)
                    shared_out(i)

            pe.wait_ge(const_made, 6)
            pe.wait_ge(w_small, 16 * SMALL)
            pe.wait_ge(start_split, 1)
            batch(0, False)
            pe.wait_ge(start_split, 2)
            with pe.Fori(1, NB) as i:
                batch(i, True)
            y_product(NB)
            t2(NB)
            t3(NB)
            mlp_in(NB)
            mlp_down(NB)
            project(NB)
            t4(NB)
            gate(NB)
            shared_in(NB)
            counts(NB)
            shared_out(NB)

            def rows_in(q, k, landed):
                pe.wait_ge(rows_landed[k], landed)
                for e in range(2):
                    for r in range(2):
                        m = e * 2 + r
                        op = pe.transpose(banks[k][:, m * P:(m + 1) * P], rows[k][:, e, r * D:(r + 1) * D], identity[:])
                op.then_inc(rows_t_full, 1)

            def gate_up(q, k):
                pe.wait_ge(rows_t_ready, q + 1)
                for e in range(2):
                    op = pe.matmul(banks[2 + k][:, e * 2 * P:(e + 1) * 2 * P], w13[k][:, e, :],
                                   rows_t[k][:, 2 * e:2 * e + 2, :], start=True, stop=True)
                op.then_inc(gu_full, 1)

            def down(q, k):
                pe.wait_ge(hidden_ready, q + 1)
                for m in range(4):
                    op = pe.matmul(banks[4 + k][:, m * D:(m + 1) * D], hidden[k][EH:P, m * P:(m + 1) * P],
                                   w2e[k][EH:P, m // 2, :], start=True, stop=True)
                op.then_inc(y_full, 1)

            pe.wait_ge(free["SW2"], NB + 1)
            rows_in(0, 0, 48)
            gate_up(0, 0)
            with pe.Fori(0, PAIRS // 2 - 1) as g:
                rows_in(g * 2 + 1, 1, g * 48 + 48)
                gate_up(g * 2 + 1, 1)
                pe.wait_ge(y_stored[0], g * 16)
                down(g * 2, 0)
                rows_in(g * 2 + 2, 0, g * 48 + 96)
                gate_up(g * 2 + 2, 0)
                pe.wait_ge(y_stored[1], g * 16)
                down(g * 2 + 1, 1)
            g = PAIRS // 2 - 1
            rows_in(g * 2 + 1, 1, g * 48 + 48)
            gate_up(g * 2 + 1, 1)
            pe.wait_ge(y_stored[0], g * 16)
            down(g * 2, 0)
            pe.wait_ge(y_stored[1], g * 16)
            down(g * 2 + 1, 1)


def kernel(**inputs):
    import numpy as np
    import concourse.bacc as bacc
    from concourse.bass_utils import run_bass_kernel_spmd

    a = {k: np.asarray(v) for k, v in inputs.items()}
    nb, s = a["x"].shape
    d = a["L0_tok_W"].shape[0]
    e, _, eh = a["L0_ffn_w1"].shape
    tiles = nb * s // P
    w13 = np.concatenate([a["L0_ffn_w1"], a["L0_ffn_w3"]], axis=2)
    laid = {
        "ids": a["x"].reshape(tiles, P).T,
        "embed": a["L0_tok_W"].T,
        "pT": a["L0_attn_P"].transpose(2, 0, 1),
        "qT": a["L0_attn_Q"].transpose(2, 0, 1),
        "gamma": a["L0_attn_gamma"].reshape(d, 1),
        "beta": a["L0_attn_beta"].reshape(d, 1),
        "w1T": a["L0_attn_W1"].T,
        "b1": a["L0_attn_b1"].reshape(2, d).T,
        "w2T": a["L0_attn_W2"].T.reshape(2, d, d).transpose(1, 0, 2),
        "b2": a["L0_attn_b2"].reshape(d, 1),
        "wpT": a["L0_attn_Wp"].T,
        "bp": a["L0_attn_bp"].reshape(1, d),
        "gateT": a["L0_ffn_gate_w"].T,
        "ew13": w13.reshape(e // 2, 2, d, 2 * eh).transpose(0, 2, 1, 3),
        "ew2": a["L0_ffn_w2"].reshape(e // 2, 2, eh, d).transpose(0, 2, 1, 3),
        "sw1": a["L0_ffn_sw1"],
        "sw3": a["L0_ffn_sw3"],
        "sw2": a["L0_ffn_sw2"],
    }
    nc = bacc.Bacc("TRN2", target_bir_lowering=False, num_devices=1)
    arrays, args = {}, []
    for name, v in laid.items():
        v = np.ascontiguousarray(v)
        arrays[f"in_{name}"] = v
        args.append(nc.dram_tensor(f"in_{name}", v.shape, mybir.dt.from_np(v.dtype), kind="ExternalInput").ap())
    args.append(nc.dram_tensor("out_0", (nb, s, d), F32, kind="ExternalOutput").ap())
    tower(nc, *args)
    r = run_bass_kernel_spmd(nc, [arrays], core_ids=[0])
    return r.results[0]["out_0"]
```

```python
from contextlib import ExitStack

import concourse.bass as bass
from concourse import mybir
from concourse.alu_op_type import AluOpType as ALU

ACT = mybir.ActivationFunctionType
AXES = mybir.AxisListType
F32 = mybir.dt.float32
F32R = mybir.dt.float32r
BF16 = mybir.dt.bfloat16
I32 = mybir.dt.int32
U32 = mybir.dt.uint32

P = 128

TOP_K = 2
CAP = 256
ROUTE_SCALE = 2.5
LN_EPS = 1e-5
PADDING_IDX = 0
DROPPED = 1 << 20

HEADS = 8
GROUPS = 8
FRONT = ["T1"] + [f"Q{_h}" for _h in range(HEADS)] + ["SC0", "X", "SC1"]
for _k in range(GROUPS - 2):
    FRONT += [f"SC{_k + 2}", f"U{_k}"]
FRONT += ["U6", "U7"]
BACK = ["Y", "T2", "T3", "W1a", "W1b", "W2", "WP", "T4", "G", "S1", "S3", "C", "SW2"]
NF = len(FRONT)
FRONT_BANKS = 5
BACK_BANKS = 3


def front_bank(name):
    return FRONT.index(name) % FRONT_BANKS


def front_before(name):
    at = FRONT.index(name)
    if at >= FRONT_BANKS:
        return at - FRONT_BANKS + 1
    last = max(k for k in range(NF) if k % FRONT_BANKS == at)
    return last + 1 - NF


def back_bank(name):
    return FRONT_BANKS + BACK.index(name) % BACK_BANKS


def back_before(name):
    at = BACK.index(name)
    if at >= BACK_BANKS:
        return BACK[at - BACK_BANKS], False
    last = max(k for k in range(len(BACK)) if k % BACK_BANKS == at)
    return BACK[last], True


def tower(nc, ids, embed, pT, qT, gamma, beta, w1T, b1, w2T, b2, wpT, bp, gateT, ew13, ew2, sw1, sw3, sw2, out):
    NB, S, D = out.shape
    C = S // P
    TILES = NB * C
    H = qT.shape[1]
    E = gateT.shape[1]
    EH = ew2.shape[1]
    PAIRS = E // 2
    SLOTS = E * CAP
    HG = H // 2
    SCORE_SCALE = 1.0 / (H * float(D) ** 0.5)
    assert D == P and C == 4 and H == HEADS and H * C // HG == GROUPS and CAP == 2 * P and EH == P // 2

    out_v = out.rearrange("b (c p) d -> b p c d", p=P)
    xbuf = nc.dram_tensor("expert_rows_in", (SLOTS, D), F32, kind="Internal").ap()
    ybuf = nc.dram_tensor("expert_rows_out", (SLOTS, D), F32, kind="Internal").ap()
    xbuf_v = xbuf.rearrange("(q e p r) d -> q p e (r d)", e=2, p=P, r=2)
    ybuf_v = ybuf.rearrange("(q e p r) d -> q p e (r d)", e=2, p=P, r=2)
    ZW = 1024
    PLACES = 4
    xbuf_z = xbuf.rearrange("(z p r) d -> z p (r d)", p=P, r=ZW // D)
    NZ = SLOTS * D // (P * ZW)

    ctx = ExitStack()
    with ctx:
        def sb(name, shape, dt=F32):
            return ctx.enter_context(nc.sbuf_tensor(name, shape, dt))

        def sem(name):
            return ctx.enter_context(nc.semaphore(name))

        identity = sb("identity", [P, P])
        upper = sb("upper", [P, P], BF16)
        ones = sb("ones", [P, P], BF16)
        expert_iota = sb("expert_iota", [P, E])
        minus_half = sb("minus_half", [P, C])
        zeros = sb("zeros", [P, ZW])
        ids_sb = sb("ids_sb", [P, TILES], I32)
        not_pad = sb("not_pad", [P, TILES])
        raw_q, raw_p = sb("raw_q", [P, H, D]), sb("raw_p", [P, H, D])
        q_hi, q_lo = sb("q_hi", [P, H, D], F32R), sb("q_lo", [P, H, D], F32R)
        p_hi, p_lo = sb("p_hi", [P, H, D], F32R), sb("p_lo", [P, H, D], F32R)
        gamma_sb, beta_sb, b2_sb = sb("gamma_sb", [P, 1]), sb("beta_sb", [P, 1]), sb("b2_sb", [P, 1])
        b1_sb = sb("b1_sb", [P, 2])
        bp_sb = sb("bp_sb", [P, D])
        w1_sb, w2_sb, wp_sb = sb("w1_sb", [P, 2 * D]), sb("w2_sb", [P, 2, D]), sb("wp_sb", [P, D])
        gate_sb = sb("gate_sb", [P, E])
        sw1_sb, sw3_sb, sw2_sb = sb("sw1_sb", [P, D]), sb("sw3_sb", [P, D]), sb("sw2_sb", [P, D])

        stream = sb("stream", [P, TILES, D])
        pair_slot = sb("pair_slot", [P, NB, TOP_K * C], I32)
        pair_weight = sb("pair_weight", [P, NB, TOP_K * C])

        ids_now = sb("ids_now", [P, C], I32)
        gathered = sb("gathered", [P, C, D])
        emb = sb("emb", [P, C, D])
        stats1, mv1 = sb("stats1", [P, C, 6]), sb("mv1", [P, C, 2])
        var1, rstd1, shift1 = sb("var1", [P, C]), sb("rstd1", [P, C]), sb("shift1", [P, C])
        xn = sb("xn", [P, C, D])
        x_hi, x_lo = sb("x_hi", [P, C, D], F32R), sb("x_lo", [P, C, D], F32R)
        xt_hi, xt_lo = sb("xt_hi", [P, S], F32R), sb("xt_lo", [P, S], F32R)
        xt = sb("xt", [P, S])
        state = sb("state", [P, C - 1, D])
        st_hi, st_lo = sb("st_hi", [P, C - 1, D], F32R), sb("st_lo", [P, C - 1, D], F32R)
        qz_hi, qz_lo = sb("qz_hi", [P, H, S], F32R), sb("qz_lo", [P, H, S], F32R)
        sc_hi, sc_lo = sb("sc_hi", [P, 4, HG, P], F32R), sb("sc_lo", [P, 4, HG, P], F32R)
        ut_hi, ut_lo = sb("ut_hi", [P, H, S], F32R), sb("ut_lo", [P, H, S], F32R)
        vt = sb("vt", [P, S])
        stats2, mv2 = sb("stats2", [P, C, 6]), sb("mv2", [P, C, 2])
        var2, rstd2, shift2 = sb("var2", [P, C]), sb("rstd2", [P, C]), sb("shift2", [P, C])
        z0 = sb("z0", [P, C, D])
        zt = sb("zt", [P, S])
        m1 = sb("m1", [P, 2, S])
        z2t = sb("z2t", [P, S])
        stats3, mv3 = sb("stats3", [P, C, 6]), sb("mv3", [P, C, 2])
        var3, rstd3, shift3 = sb("var3", [P, C]), sb("rstd3", [P, C]), sb("shift3", [P, C])
        xf = sb("xf", [P, C, D])
        xft = sb("xft", [P, S])
        scores = sb("scores", [P, C, E])
        top8, index8 = sb("top8", [P, C, 8]), sb("index8", [P, C, 8], U32)
        index2 = sb("index2", [P, TOP_K, C])
        chosen = sb("chosen", [P, TOP_K, C, E])
        chosen_pos = sb("chosen_pos", [P, TOP_K, C, E])
        either = sb("either", [P, C, E], BF16)
        seen, seen_new = sb("seen", [P, E], BF16), sb("seen_new", [P, E])
        pos = sb("pos", [P, TOP_K, C])
        kept = sb("kept", [P, TOP_K, C])
        pos_in = sb("pos_in", [P, TOP_K, C])
        slot_f = sb("slot_f", [P, TOP_K, C])
        slot_drop = sb("slot_drop", [P, TOP_K, C])
        slot_out = sb("slot_out", [P, TOP_K * C], I32)
        top_sum, top_inv = sb("top_sum", [P, C]), sb("top_inv", [P, C])
        weight = sb("weight", [P, TOP_K, C])
        sig, gated, hs = sb("sig", [P, S]), sb("gated", [P, S]), sb("hs", [P, S])
        rows = [sb(f"rows{k}", [P, 2, 2 * D]) for k in range(PLACES)]
        w13 = [sb(f"w13_{k}", [P, 2, P]) for k in range(PLACES)]
        w2e = [sb(f"w2e_{k}", [P, 2, D]) for k in range(PLACES)]
        y_sb = [sb(f"y_sb{k}", [P, 2, 2 * D]) for k in range(PLACES)]
        rows_t = [m1[:, k, :].rearrange("p (m s) -> p m s", s=P) for k in range(2)]
        silu = [sig, gated]
        hidden = [hs, z2t]
        slot_now = [sb(f"slot_now{k}", [P, TOP_K * C], I32) for k in range(2)]
        y_got = [raw_q, raw_p]

        banks = [ctx.enter_context(nc.psum_tensor(f"bank{k}", [P, S], F32)) for k in range(8)]

        wait_carried = sem("wait_carried")
        w_q = sem("w_q_landed")
        w_p = sem("w_p_landed")
        w_bp = sem("bp_landed")
        w_small = sem("small_weights_landed")
        w_ids = sem("ids_landed")
        const_made = sem("constants_made")
        const_step = sem("constant_begun")
        q_hi_made, q_lo_made = sem("q_hi_made"), sem("q_lo_made")
        p_hi_made, p_lo_made = sem("p_hi_made"), sem("p_lo_made")
        pad_made = sem("pad_mask_made")
        zero_made = sem("zeros_made")
        zero_filled = sem("expert_rows_zeroed")
        ids_copied = sem("ids_copied")
        emb_landed = sem("embeddings_landed")
        emb_masked = sem("embeddings_masked")
        stream_begun = sem("stream_begun")
        ln1_stats, ln1_mean, ln1_var = sem("ln1_stats"), sem("ln1_mean"), sem("ln1_var")
        ln1_rstd, ln1_shift, xn_ready = sem("ln1_rstd"), sem("ln1_shift"), sem("xn_ready")
        x_hi_ready, x_split = sem("x_hi_ready"), sem("x_split")
        xt_ready = sem("xt_ready")
        front_full, front_hi, front_free = sem("front_full"), sem("front_hi"), sem("front_free")
        state_step, state_hi, state_split = sem("state_step"), sem("state_hi"), sem("state_split")
        masked = sem("scores_masked")
        full = {n: sem(f"{n}_full") for n in BACK}
        free = {n: sem(f"{n}_free") for n in BACK}
        ln2_stats, ln2_mean, ln2_var = sem("ln2_stats"), sem("ln2_mean"), sem("ln2_var")
        ln2_rstd, ln2_shift = sem("ln2_rstd"), sem("ln2_shift")
        ln3_stats, ln3_mean, ln3_var = sem("ln3_stats"), sem("ln3_mean"), sem("ln3_var")
        ln3_rstd, ln3_shift, xf_ready = sem("ln3_rstd"), sem("ln3_shift"), sem("xf_ready")
        top_found, index_found, index_float = sem("top_found"), sem("index_found"), sem("index_float")
        chosen_made, either_made = sem("chosen_made"), sem("either_made")
        seen_sum, seen_made = sem("seen_sum"), sem("seen_made")
        pos_made, kept_made, slot_made = sem("pos_made"), sem("kept_made"), sem("slot_made")
        slots_ready, rows_sent = sem("slots_ready"), sem("rows_sent")
        weight_step, weight_ready = sem("weight_step"), sem("weight_ready")
        sig_ready, gated_ready = sem("sig_ready"), sem("gated_ready")
        rows_landed = [sem(f"rows_landed{k}") for k in range(PLACES)]
        w13_landed = [sem(f"w13_landed{k}") for k in range(PLACES)]
        w2_landed = [sem(f"w2_landed{k}") for k in range(PLACES)]
        rows_t_full, rows_t_ready = sem("rows_t_full"), sem("rows_t_ready")
        gu_full, silu_ready, hidden_ready = sem("gu_full"), sem("silu_ready"), sem("hidden_ready")
        y_full, y_ready = sem("y_full"), sem("y_ready")
        y_stored = [sem(f"y_stored{k}") for k in range(PLACES)]
        slot_copied = sem("slot_copied")
        y_landed = [sem(f"y_landed{k}") for k in range(2)]
        pair_added, tiles_done = sem("pair_added"), sem("tiles_done")
        out_stored = sem("out_stored")

        SMALL = 11
        block = ctx.enter_context(nc.Block())

        def wait(eng, s, value):
            if not (isinstance(value, int) and value <= 0):
                eng.wait_ge(s, value)

        def carried(eng):
            eng.sem_inc(wait_carried, 1)

        def tile_slice(i):
            return bass.ds(i * C, C)

        @block.sync
        def _(sp):
            sp.dma_start(ids_sb[:], ids).then_inc(w_ids, 16)
            sp.dma_start(raw_q[:], qT).then_inc(w_q, 16)
            sp.dma_start(bp_sb[:], bp.broadcast_to([P, D])).then_inc(w_bp, 16)
            sp.dma_start(raw_p[:], pT).then_inc(w_p, 16)
            for dst, src in ((gamma_sb[:], gamma), (beta_sb[:], beta), (b1_sb[:], b1), (b2_sb[:], b2),
                             (w1_sb[:], w1T), (w2_sb[:], w2T), (wp_sb[:], wpT), (gate_sb[:], gateT),
                             (sw1_sb[:], sw1), (sw3_sb[:], sw3), (sw2_sb[:], sw2)):
                sp.dma_start(dst, src).then_inc(w_small, 16)
            sp.wait_ge(zero_made, 1)
            with sp.Fori(0, NZ) as z:
                sp.dma_start(xbuf_z[bass.ds(z, 1)].rearrange("z p n -> p (z n)"), zeros[:]).then_inc(zero_filled, 16)

            def load_rows(q, k):
                wait(sp, rows_t_full, q - (PLACES - 1))
                sp.dma_start(rows[k][:], xbuf_v[bass.ds(q, 1)].rearrange("q p e n -> p (q e) n")).then_inc(rows_landed[k], 16)

            def load_w13(q, k):
                wait(sp, gu_full, q - (PLACES - 1))
                sp.dma_start(w13[k][:], ew13[bass.ds(q, 1)].rearrange("q p e f -> p (q e) f")).then_inc(w13_landed[k], 16)

            def load_w2(q, k):
                wait(sp, y_full, q - (PLACES - 1))
                sp.dma_start(w2e[k][EH:P], ew2[bass.ds(q, 1)].rearrange("q f e d -> f (q e) d")).then_inc(w2_landed[k], 16)

            for k in range(PLACES):
                load_w13(k, k)
                load_w2(k, k)
            sp.wait_ge(rows_sent, 16 * TILES * TOP_K)
            for k in range(PLACES):
                load_rows(k, k)
            with sp.Fori(1, PAIRS // PLACES) as g:
                for k in range(PLACES):
                    load_rows(g * PLACES + k, k)
                    load_w13(g * PLACES + k, k)
                    if k >= 2:
                        load_w2(g * PLACES + k - 2, k - 2)
                load_w2(g * PLACES + 2, 2)
                load_w2(g * PLACES + 3, 3)

            with sp.Fori(0, NB) as i:
                sp.wait_ge(tiles_done, i + 1)
                sp.dma_start(out_v[bass.ds(i, 1)].rearrange("b p c d -> p (b c) d"), stream[:, tile_slice(i), :]).then_inc(out_stored, 16)
            sp.wait_ge(out_stored, 16 * NB)

        @block.gpsimd
        def _(pool):
            pool.memset(zeros[:], 0.0).then_inc(zero_made, 1)
            pool.memset(identity[:], 0.0).then_inc(const_step, 1)
            pool.memset(upper[:], 1.0).then_inc(const_step, 1)
            pool.memset(ones[:], 1.0).then_inc(const_made, 1)
            pool.memset(minus_half[:], -0.5).then_inc(const_made, 1)
            pool.memset(seen[:], 0.0).then_inc(const_made, 1)
            pool.iota(expert_iota[:], pattern=[[1, E]], base=0, channel_multiplier=0,
                      allow_small_or_imprecise_dtypes=True).then_inc(const_made, 1)
            pool.wait_ge(const_step, 2)
            pool.affine_select(out=identity[:], in_=identity[:], compare_op=ALU.not_equal, fill=1.0,
                               base=0, pattern=[[-1, P]], channel_multiplier=1).then_inc(const_made, 1)
            pool.affine_select(out=upper[:], in_=upper[:], compare_op=ALU.is_gt, fill=0.0,
                               base=0, pattern=[[1, P]], channel_multiplier=-1).then_inc(const_made, 1)

            def gather(i, c):
                if c == 0:
                    wait(pool, emb_landed, i * (16 * C))
                    pool.tensor_copy(ids_now[:], ids_sb[:, tile_slice(i)]).then_inc(ids_copied, 1)
                    pool.wait_ge(ids_copied, i + 1)
                    wait(pool, emb_masked, i * C)
                    carried(pool)
                pool.indirect_dma_start(
                    out=gathered[:, c, :], out_offset=None, in_=embed,
                    in_offset=bass.IndirectOffsetOnAxis(ap=ids_now[:, c:c + 1], axis=0)).then_inc(emb_landed, 16)

            def inverse_deviation(out_ap, var, var_ready, ready, n):
                pool.wait_ge(var_ready, n)
                pool.tensor_tensor(out_ap[:], var[:], minus_half[:], ALU.pow).then_inc(ready, 1)

            def begin_stream(i):
                pool.wait_ge(emb_masked, i * C + C)
                pool.tensor_tensor(stream[:, tile_slice(i), :], emb[:],
                                   bp_sb[:].unsqueeze(1).broadcast_to([P, C, D]), ALU.add).then_inc(stream_begun, 1)

            def x_low(i):
                pool.wait_ge(x_hi_ready, i + 1)
                pool.tensor_tensor(x_lo[:], xn[:], x_hi[:].bitcast(F32), ALU.subtract).then_inc(x_split, 1)

            def state_low(i):
                pool.wait_ge(state_hi, i + 1)
                pool.tensor_tensor(st_lo[:], state[:], st_hi[:].bitcast(F32), ALU.subtract).then_inc(state_split, 1)

            def mask(i, k):
                pool.wait_ge(front_free, i * NF + FRONT.index(f"SC{k}") + 1)
                carried(pool)
                pool.affine_select(out=sc_hi[:, k % 4], in_=sc_hi[:, k % 4].bitcast(F32), compare_op=ALU.is_ge,
                                   fill=0.0, base=0, pattern=[[0, HG], [1, P]], channel_multiplier=-1)
                pool.affine_select(out=sc_lo[:, k % 4], in_=sc_lo[:, k % 4].bitcast(F32), compare_op=ALU.is_ge,
                                   fill=0.0, base=0, pattern=[[0, HG], [1, P]], channel_multiplier=-1).then_inc(masked, 1)

            def dispatch(n):
                pool.wait_ge(slots_ready, n)
                carried(pool)
                for m in range(TOP_K * C):
                    pool.indirect_dma_start(
                        out=xbuf, out_offset=bass.IndirectOffsetOnAxis(ap=slot_out[:, m:m + 1], axis=0),
                        in_=xf[:, m % C, :], in_offset=None,
                        bounds_check=SLOTS - 1, oob_is_err=False).then_inc(rows_sent, 16)

            def batch(i, more, behind):
                if behind:
                    inverse_deviation(rstd2, var2, ln2_var, ln2_rstd, i)
                for k in range(GROUPS):
                    mask(i, k)
                    if k == 1:
                        state_low(i)
                    if k < C and more:
                        gather(i + 1, k)
                    if k == 4 and behind:
                        inverse_deviation(rstd3, var3, ln3_var, ln3_rstd, i)
                    if k == 6 and more:
                        inverse_deviation(rstd1, var1, ln1_var, ln1_rstd, i + 2)
                if more:
                    begin_stream(i + 1)
                    x_low(i + 1)
                if behind:
                    dispatch(i)

            pool.wait_ge(w_ids, 16)
            for c in range(C):
                gather(0, c)
            inverse_deviation(rstd1, var1, ln1_var, ln1_rstd, 1)
            pool.wait_ge(w_bp, 16)
            begin_stream(0)
            x_low(0)
            batch(0, True, False)
            pool.wait_ge(zero_filled, 16 * NZ)
            with pool.Fori(1, NB - 1) as i:
                batch(i, True, True)
            batch(NB - 1, False, True)
            inverse_deviation(rstd2, var2, ln2_var, ln2_rstd, NB)
            inverse_deviation(rstd3, var3, ln3_var, ln3_rstd, NB)
            dispatch(NB)

            def fetch(i, k):
                wait(pool, tiles_done, i - 1)
                pool.tensor_copy(slot_now[k][:], pair_slot[:, bass.ds(i, 1), :].rearrange("p b m -> p (b m)")).then_inc(slot_copied, 1)
                pool.wait_ge(slot_copied, i + 1)
                carried(pool)
                for m in range(TOP_K * C):
                    pool.indirect_dma_start(
                        out=y_got[k][:, m, :], out_offset=None, in_=ybuf,
                        in_offset=bass.IndirectOffsetOnAxis(ap=slot_now[k][:, m:m + 1], axis=0)).then_inc(y_landed[k], 16)

            for k in range(PLACES):
                pool.wait_ge(y_stored[k], 16 * PAIRS // PLACES)
            pool.wait_ge(weight_ready, NB)
            fetch(0, 0)
            fetch(1, 1)
            with pool.Fori(1, NB // 2) as g:
                for k in range(2):
                    fetch(g * 2 + k, k)

        @block.scalar
        def _(act):
            act.preload_act_table(ACT.Sigmoid)

            def embed_in(i):
                act.wait_ge(emb_landed, i * (16 * C) + 16 * C)
                wait(act, xn_ready, i * C)
                wait(act, stream_begun, i)
                for c in range(C):
                    act.activation(emb[:, c, :], gathered[:, c, :], ACT.Copy,
                                   scale=not_pad[:, bass.ds(i * C + c, 1)]).then_inc(emb_masked, 1)

            def normalise(i):
                act.wait_ge(ln1_shift, i + 1)
                wait(act, x_split, i)
                for c in range(C):
                    act.activation(xn[:, c, :], emb[:, c, :], ACT.Identity, scale=rstd1[:, c:c + 1],
                                   bias=shift1[:, c:c + 1]).then_inc(xn_ready, 1)

            def x_high(i):
                wait(act, front_full, i * NF)
                act.wait_ge(xn_ready, i * C + C)
                act.copy(x_hi[:], xn[:]).then_inc(x_hi_ready, 1)

            def leading(i, name, dst, scale=1.0):
                b = banks[front_bank(name)]
                act.wait_ge(front_full, i * NF + FRONT.index(name) + 1)
                src = b[:] if len(dst.shape) == 2 else b[:].rearrange("p (a b) -> p a b", b=P)
                act.activation(dst, src, ACT.Copy, scale=scale).then_inc(front_hi, 1)

            def keep_xt(i):
                wait(act, free["Y"], i)
                act.copy(xt[:], banks[front_bank("T1")][:]).then_inc(xt_ready, 1)

            def ln_mid_apply(n):
                act.wait_ge(ln2_shift, n)
                for c in range(C):
                    op = act.activation(z0[:, c, :], banks[back_bank("T2")][:, c * D:(c + 1) * D], ACT.Identity,
                                        scale=rstd2[:, c:c + 1], bias=shift2[:, c:c + 1])
                op.then_inc(free["T2"], 1)

            def gamma_beta(n):
                act.wait_ge(full["T3"], n)
                act.activation(zt[:], banks[back_bank("T3")][:], ACT.Identity, bias=beta_sb[:], scale=gamma_sb[:]).then_inc(free["T3"], 1)

            def relu(n, j):
                name = "W1a" if j == 0 else "W1b"
                act.wait_ge(full[name], n)
                act.activation(m1[:, j, :], banks[back_bank(name)][:], ACT.Relu, bias=b1_sb[:, j:j + 1]).then_inc(free[name], 1)

            def ln_last_apply(n, i):
                act.wait_ge(ln3_shift, n)
                wait(act, rows_sent, (n - 1) * (16 * TOP_K * C))
                for c in range(C):
                    op = act.activation(xf[:, c, :], stream[:, bass.ds(i * C + c, 1), :].rearrange("p a d -> p (a d)"),
                                        ACT.Identity, scale=rstd3[:, c:c + 1], bias=shift3[:, c:c + 1])
                op.then_inc(xf_ready, 1)

            def copy_xft(n):
                act.wait_ge(full["T4"], n)
                act.activation(xft[:], banks[back_bank("T4")][:], ACT.Copy).then_inc(free["T4"], 1)

            def gate_sigmoid(n):
                act.wait_ge(full["G"], n)
                act.activation(scores[:], banks[back_bank("G")][:, 0:C * E].rearrange("p (c e) -> p c e", e=E),
                               ACT.Sigmoid).then_inc(free["G"], 1)

            def shared_sigmoid(n):
                act.wait_ge(full["S1"], n)
                act.activation(sig[:], banks[back_bank("S1")][:], ACT.Sigmoid).then_inc(sig_ready, 1)

            def batch(i, more, behind):
                leading(i, "T1", xt_hi[:])
                leading(i, "Q0", qz_hi[:, 0, :], SCORE_SCALE)
                keep_xt(i)
                for name in FRONT[FRONT.index("Q1"):]:
                    k = int(name[-1]) if name != "X" else 0
                    if name.startswith("Q"):
                        leading(i, name, qz_hi[:, k, :], SCORE_SCALE)
                        if name == "Q5" and behind:
                            ln_mid_apply(i)
                    elif name.startswith("SC"):
                        leading(i, name, sc_hi[:, k % 4])
                        if name == "SC1":
                            act.wait_ge(state_step, i * 3 + 3)
                            act.copy(st_hi[:], state[:]).then_inc(state_hi, 1)
                            if behind:
                                gamma_beta(i)
                        if name == "SC2" and behind:
                            relu(i, 0)
                            relu(i, 1)
                        if name == "SC5" and more:
                            embed_in(i + 1)
                        if name == "SC6" and behind:
                            ln_last_apply(i, i - 1)
                        if name == "SC7" and behind:
                            copy_xft(i)
                    elif name.startswith("U"):
                        c, g = k // 2, k % 2
                        leading(i, name, ut_hi[:, HG * g:HG * g + HG, c * P:(c + 1) * P])
                        if name == "U5" and behind:
                            gate_sigmoid(i)
                            shared_sigmoid(i)
                        if name == "U6" and more:
                            normalise(i + 1)
                if more:
                    x_high(i + 1)

            act.wait_ge(pad_made, 1)
            embed_in(0)
            act.wait_ge(w_q, 16)
            act.copy(q_hi[:], raw_q[:]).then_inc(q_hi_made, 1)
            normalise(0)
            x_high(0)
            act.wait_ge(w_p, 16)
            act.copy(p_hi[:], raw_p[:]).then_inc(p_hi_made, 1)
            batch(0, True, False)
            act.wait_ge(w_small, 16 * SMALL)
            with act.Fori(1, NB - 1) as i:
                batch(i, True, True)
            batch(NB - 1, False, True)
            ln_mid_apply(NB)
            gamma_beta(NB)
            relu(NB, 0)
            relu(NB, 1)
            ln_last_apply(NB, NB - 1)
            copy_xft(NB)
            gate_sigmoid(NB)
            shared_sigmoid(NB)

            def silu_of(q, k):
                act.wait_ge(gu_full, q + 1)
                wait(act, hidden_ready, q - 1)
                act.activation(silu[k % 2][EH:P, :], banks[2 + k][0:EH, :], ACT.Silu).then_inc(silu_ready, 1)

            def y_out(q, k):
                act.wait_ge(y_full, q + 1)
                wait(act, y_stored[k], q * (16 // PLACES) - k * (16 // PLACES))
                act.activation(y_sb[k][:].rearrange("p e n -> p (e n)"), banks[6 + k % 2][:], ACT.Copy).then_inc(y_ready, 1)

            def y_store(q, k):
                act.wait_ge(y_ready, q + 1)
                act.dma_start(ybuf_v[bass.ds(q, 1)].rearrange("q p e n -> p (q e) n"), y_sb[k][:]).then_inc(y_stored[k], 16)

            def expert_step(p, k, first=False):
                if not (isinstance(p, int) and p + 2 >= PAIRS):
                    silu_of(p + 2, (k + 2) % PLACES)
                y_out(p, k)
                if not (isinstance(p, int) and p == 0):
                    y_store(p - 1, (k - 1) % PLACES)

            silu_of(0, 0)
            silu_of(1, 1)
            for p in range(PLACES):
                expert_step(p, p)
            with act.Fori(1, PAIRS // PLACES - 1) as g:
                for k in range(PLACES):
                    expert_step(g * PLACES + k, k)
            for k in range(PLACES):
                expert_step(PAIRS - PLACES + k, k)
            y_store(PAIRS - 1, PLACES - 1)

        @block.vector
        def _(dve):
            dve.wait_ge(w_ids, 16)
            dve.tensor_scalar(not_pad[:], ids_sb[:], float(PADDING_IDX), None, ALU.not_equal).then_inc(pad_made, 1)
            for name in BACK:
                if name in [back_before(x)[0] for x in BACK if back_before(x)[1]]:
                    dve.sem_inc(free[name], 1)

            dve.sem_inc(seen_made, 1)

            def mean_var(stats, mv, var, source, s_stats, s_mean, s_var, n):
                carried(dve)
                for c in range(C):
                    dve.bn_stats(stats[:, c, :], source[:, c, :]).then_inc(s_stats, 1)
                dve.wait_ge(s_stats, n * C)
                carried(dve)
                for c in range(C):
                    dve.bn_aggr(mv[:, c, :], stats[:, c, :]).then_inc(s_mean, 1)
                dve.wait_ge(s_mean, n * C)
                dve.tensor_scalar(var[:], mv[:, :, 1], LN_EPS, None, ALU.add).then_inc(s_var, 1)

            def shift(out_ap, mv, rstd, rstd_ready, ready, n):
                dve.wait_ge(rstd_ready, n)
                dve.scalar_tensor_tensor(out_ap[:], mv[:, :, 0], -1.0, rstd[:], ALU.mult, ALU.mult).then_inc(ready, 1)

            def ln_first(i):
                dve.wait_ge(emb_masked, i * C + C)
                mean_var(stats1, mv1, var1, emb, ln1_stats, ln1_mean, ln1_var, i + 1)

            def rest(i, name, hi, lo, scale=1.0):
                b = banks[front_bank(name)]
                at = FRONT.index(name)
                dve.wait_ge(front_hi, i * (NF - 1) + (at + 1 if at < FRONT.index("X") else at))
                src = b[:] if len(hi.shape) == 2 else b[:].rearrange("p (a b) -> p a b", b=P)
                dve.scalar_tensor_tensor(lo, src, scale, hi.bitcast(F32), ALU.mult, ALU.subtract).then_inc(front_free, 1)

            def states(i):
                b = banks[front_bank("X")]
                dve.wait_ge(front_full, i * NF + FRONT.index("X") + 1)
                wait(dve, state_split, i)
                dve.tensor_copy(state[:, 0, :], b[:, 0:D]).then_inc(state_step, 1)
                dve.wait_ge(state_step, i * 3 + 1)
                dve.tensor_tensor(state[:, 1, :], state[:, 0, :], b[:, D:2 * D], ALU.add).then_inc(state_step, 1)
                dve.wait_ge(state_step, i * 3 + 2)
                dve.tensor_tensor(state[:, 2, :], state[:, 1, :], b[:, 2 * D:3 * D], ALU.add).then_inc(state_step, 1)
                dve.wait_ge(state_step, i * 3 + 3)
                dve.sem_inc(front_free, 1)

            def residual(n):
                dve.wait_ge(full["Y"], n)
                dve.wait_ge(xt_ready, n)
                dve.tensor_tensor(vt[:], banks[back_bank("Y")][:], xt[:], ALU.add).then_inc(free["Y"], 1)

            def ln_mid(n):
                dve.wait_ge(full["T2"], n)
                v = banks[back_bank("T2")][:].rearrange("p (c d) -> p c d", d=D)
                mean_var(stats2, mv2, var2, v, ln2_stats, ln2_mean, ln2_var, n)

            def mlp_out(n):
                dve.wait_ge(full["W2"], n)
                dve.scalar_tensor_tensor(z2t[:], banks[back_bank("W2")][:], b2_sb[:], zt[:], ALU.add, ALU.add).then_inc(free["W2"], 1)

            def attn_out(n, i):
                dve.wait_ge(full["WP"], n)
                dve.wait_ge(stream_begun, n)
                h = stream[:, tile_slice(i), :]
                dve.tensor_tensor(h, banks[back_bank("WP")][:].rearrange("p (c d) -> p c d", d=D), h, ALU.add).then_inc(free["WP"], 1)

            def ln_last(n, i):
                dve.wait_ge(free["WP"], n)
                carried(dve)
                for c in range(C):
                    dve.bn_stats(stats3[:, c, :], stream[:, bass.ds(i * C + c, 1), :].rearrange("p a d -> p (a d)")).then_inc(ln3_stats, 1)
                dve.wait_ge(ln3_stats, n * C)
                carried(dve)
                for c in range(C):
                    dve.bn_aggr(mv3[:, c, :], stats3[:, c, :]).then_inc(ln3_mean, 1)
                dve.wait_ge(ln3_mean, n * C)
                dve.tensor_scalar(var3[:], mv3[:, :, 1], LN_EPS, None, ALU.add).then_inc(ln3_var, 1)

            def choose(n):
                dve.wait_ge(free["G"], n)
                carried(dve)
                for c in range(C):
                    dve.max(top8[:, c, :], scores[:, c, :]).then_inc(top_found, 1)
                dve.wait_ge(top_found, n * C)
                carried(dve)
                for c in range(C):
                    dve.max_index(index8[:, c, :], top8[:, c, :], scores[:, c, :]).then_inc(index_found, 1)
                dve.wait_ge(index_found, n * C)
                dve.tensor_copy(index2[:], index8[:, :, 0:TOP_K].rearrange("p c k -> p k c")).then_inc(index_float, 1)
                dve.wait_ge(index_float, n)
                dve.tensor_tensor(chosen[:], index2[:].unsqueeze(3).broadcast_to([P, TOP_K, C, E]),
                                  expert_iota[:].unsqueeze(1).unsqueeze(1).broadcast_to([P, TOP_K, C, E]),
                                  ALU.is_equal).then_inc(chosen_made, 1)
                dve.wait_ge(chosen_made, n)
                dve.tensor_tensor(either[:], chosen[:, 0], chosen[:, 1], ALU.add).then_inc(either_made, 1)
                dve.wait_ge(either_made, n)

            def route(n, i):
                dve.wait_ge(full["C"], n)
                before = banks[back_bank("C")][:, 0:C * E].rearrange("p (c e) -> p c e", e=E)
                for k in range(TOP_K):
                    op = dve.tensor_tensor(chosen_pos[:, k], before, chosen[:, k], ALU.mult)
                    op.then_inc(pos_made, 1)
                dve.sem_inc(free["C"], 1)
                dve.tensor_reduce(seen_new[:], either[:].rearrange("p c e -> p e c"), AXES.X, ALU.add).then_inc(seen_sum, 1)
                dve.wait_ge(pos_made, n * 3 - 1)
                dve.tensor_reduce(pos[:], chosen_pos[:], AXES.X, ALU.add).then_inc(pos_made, 1)
                dve.wait_ge(seen_sum, n)
                dve.tensor_tensor(seen[:], seen[:], seen_new[:], ALU.add).then_inc(seen_made, 1)
                dve.wait_ge(pos_made, n * 3)
                dve.tensor_scalar(kept[:], pos[:], float(CAP), None, ALU.is_lt).then_inc(kept_made, 1)
                dve.tensor_scalar(pos_in[:], pos[:], float(CAP - 1), None, ALU.min).then_inc(kept_made, 1)
                dve.wait_ge(kept_made, n * 2)
                dve.scalar_tensor_tensor(slot_f[:], index2[:], float(CAP), pos_in[:], ALU.mult, ALU.add).then_inc(slot_made, 1)
                dve.tensor_scalar(slot_drop[:], kept[:], -float(DROPPED), float(DROPPED), ALU.mult, ALU.add).then_inc(slot_made, 1)
                dve.wait_ge(slot_made, n * 2)
                dve.tensor_tensor(slot_out[:].rearrange("p (k c) -> p k c", c=C), slot_f[:], slot_drop[:], ALU.add).then_inc(slots_ready, 1)
                dve.tensor_copy(pair_slot[:, bass.ds(i, 1), :].rearrange("p b (k c) -> p (b k) c", c=C), slot_f[:])
                tops = top8[:, :, 0:TOP_K].rearrange("p c k -> p k c")
                dve.tensor_tensor(top_sum[:], tops[:, 0], tops[:, 1], ALU.add).then_inc(weight_step, 1)
                dve.wait_ge(weight_step, n * 4 - 3)
                dve.tensor_scalar(top_sum[:], top_sum[:], 1e-20, None, ALU.add).then_inc(weight_step, 1)
                dve.wait_ge(weight_step, n * 4 - 2)
                dve.reciprocal(top_inv[:], top_sum[:]).then_inc(weight_step, 1)
                dve.wait_ge(weight_step, n * 4 - 1)
                dve.tensor_tensor(weight[:], tops, top_inv[:].unsqueeze(1).broadcast_to([P, TOP_K, C]), ALU.mult).then_inc(weight_step, 1)
                dve.wait_ge(weight_step, n * 4)
                dve.scalar_tensor_tensor(pair_weight[:, bass.ds(i, 1), :].rearrange("p b (k c) -> p (b k) c", c=C),
                                         weight[:], ROUTE_SCALE, kept[:], ALU.mult, ALU.mult).then_inc(weight_ready, 1)

            def shared_gate(n):
                dve.wait_ge(sig_ready, n)
                dve.tensor_tensor(gated[:], banks[back_bank("S1")][:], sig[:], ALU.mult).then_inc(free["S1"], 1)
                dve.wait_ge(free["S1"], n)
                dve.wait_ge(full["S3"], n)
                dve.tensor_tensor(hs[:], banks[back_bank("S3")][:], gated[:], ALU.mult).then_inc(free["S3"], 1)

            def shared_add(n, i):
                dve.wait_ge(full["SW2"], n)
                h = stream[:, tile_slice(i), :]
                dve.tensor_tensor(h, banks[back_bank("SW2")][:].rearrange("p (c d) -> p c d", d=D), h, ALU.add).then_inc(free["SW2"], 1)

            def batch(i, more, behind):
                rest(i, "T1", xt_hi[:], xt_lo[:])
                if behind:
                    residual(i)
                for name in FRONT[FRONT.index("Q0"):]:
                    k = int(name[-1]) if name != "X" else 0
                    if name.startswith("Q"):
                        rest(i, name, qz_hi[:, k, :], qz_lo[:, k, :], SCORE_SCALE)
                        if name == "Q2" and behind:
                            ln_mid(i)
                        if name == "Q5" and behind:
                            shift(shift2, mv2, rstd2, ln2_rstd, ln2_shift, i)
                    elif name == "X":
                        states(i)
                    elif name.startswith("SC"):
                        rest(i, name, sc_hi[:, k % 4], sc_lo[:, k % 4])
                        if name == "SC3" and behind:
                            mlp_out(i)
                        if name == "SC4" and behind:
                            attn_out(i, i - 1)
                            ln_last(i, i - 1)
                        if name == "SC6" and behind:
                            shift(shift3, mv3, rstd3, ln3_rstd, ln3_shift, i)
                    else:
                        c, g = k // 2, k % 2
                        at = (slice(None), slice(HG * g, HG * g + HG), slice(c * P, (c + 1) * P))
                        rest(i, name, ut_hi[at], ut_lo[at])
                        if name == "U4" and more:
                            ln_first(i + 1)
                        if name == "U5":
                            if more:
                                shift(shift1, mv1, rstd1, ln1_rstd, ln1_shift, i + 2)
                            if behind:
                                choose(i)
                                shared_gate(i)
                if behind:
                    route(i, i - 1)
                    shared_add(i, i - 1)

            ln_first(0)
            shift(shift1, mv1, rstd1, ln1_rstd, ln1_shift, 1)
            dve.wait_ge(q_hi_made, 1)
            dve.tensor_tensor(q_lo[:], raw_q[:], q_hi[:].bitcast(F32), ALU.subtract).then_inc(q_lo_made, 1)
            dve.wait_ge(p_hi_made, 1)
            dve.tensor_tensor(p_lo[:], raw_p[:], p_hi[:].bitcast(F32), ALU.subtract).then_inc(p_lo_made, 1)
            batch(0, True, False)
            dve.wait_ge(w_small, 16 * SMALL)
            dve.wait_ge(const_made, 6)
            with dve.Fori(1, NB - 1) as i:
                batch(i, True, True)
            batch(NB - 1, False, True)
            residual(NB)
            ln_mid(NB)
            shift(shift2, mv2, rstd2, ln2_rstd, ln2_shift, NB)
            mlp_out(NB)
            attn_out(NB, NB - 1)
            ln_last(NB, NB - 1)
            shift(shift3, mv3, rstd3, ln3_rstd, ln3_shift, NB)
            choose(NB)
            shared_gate(NB)
            route(NB, NB - 1)
            shared_add(NB, NB - 1)

            def rows_out(q, k):
                dve.wait_ge(rows_t_full, q + 1)
                wait(dve, gu_full, q - 1)
                dve.tensor_copy(rows_t[k % 2], banks[k % 2][:].rearrange("p (m s) -> p m s", s=P)).then_inc(rows_t_ready, 1)

            def hidden_of(q, k):
                dve.wait_ge(silu_ready, q + 1)
                wait(dve, y_full, q - 1)
                dve.tensor_tensor(hidden[k % 2][EH:P, :], banks[2 + k][EH:P, :], silu[k % 2][EH:P, :], ALU.mult).then_inc(hidden_ready, 1)

            def expert_step(p, k):
                if not (isinstance(p, int) and p + 3 >= PAIRS):
                    rows_out(p + 3, (k + 3) % PLACES)
                if not (isinstance(p, int) and p + 2 >= PAIRS):
                    hidden_of(p + 2, (k + 2) % PLACES)

            for q in range(3):
                rows_out(q, q)
            hidden_of(0, 0)
            hidden_of(1, 1)
            for p in range(PLACES):
                expert_step(p, p)
            with dve.Fori(1, PAIRS // PLACES - 1) as g:
                for k in range(PLACES):
                    expert_step(g * PLACES + k, k)
            for k in range(PLACES):
                expert_step(PAIRS - PLACES + k, k)

            def add_pairs(i, k, landed):
                dve.wait_ge(y_landed[k], landed)
                for m in range(TOP_K * C):
                    if m == C:
                        dve.wait_ge(pair_added, i * C + C)
                    h = stream[:, bass.ds(i * C + m % C, 1), :].rearrange("p a d -> p (a d)")
                    w = pair_weight[:, bass.ds(i, 1), m:m + 1].rearrange("p a m -> p (a m)")
                    op = dve.scalar_tensor_tensor(h, y_got[k][:, m, :], w, h, ALU.mult, ALU.add)
                    if m < C:
                        op.then_inc(pair_added, 1)
                op.then_inc(tiles_done, 1)

            dve.wait_ge(weight_ready, NB)
            with dve.Fori(0, NB // 2) as g:
                for k in range(2):
                    add_pairs(g * 2 + k, k, g * (16 * TOP_K * C) + 16 * TOP_K * C)

        @block.tensor
        def _(pe):
            def product(out_ap, pairs, start=True, stop=True):
                last = None
                for n, (ah, al, bh, bl) in enumerate(pairs):
                    pe.matmul(out_ap, ah, bh, start=start and n == 0, stop=False)
                    pe.matmul(out_ap, ah, bl, start=False, stop=False)
                    last = pe.matmul(out_ap, al, bh, start=False, stop=stop and n == len(pairs) - 1)
                return last

            def front_slot(i, name):
                value = i * NF + front_before(name)
                wait(pe, front_free, value)
                return banks[front_bank(name)]

            def back_slot(n, name):
                before, _ = back_before(name)
                pe.wait_ge(free[before], n)
                return banks[back_bank(name)]

            def transposes(dst, src):
                for c in range(C):
                    op = pe.transpose(dst[:, c * P:(c + 1) * P], src(c), identity[:])
                return op

            def t1(i):
                b = front_slot(i, "T1")
                pe.wait_ge(xn_ready, i * C + C)
                transposes(b, lambda c: xn[:, c, :]).then_inc(front_full, 1)

            def qz(i, h):
                b = front_slot(i, f"Q{h}")
                product(b[:], [(q_hi[:, h, :], q_lo[:, h, :], xt_hi[:], xt_lo[:])]).then_inc(front_full, 1)

            def outer(i):
                b = front_slot(i, "X")
                pe.wait_ge(x_split, i + 1)
                for c in range(C - 1):
                    op = product(b[:, c * D:(c + 1) * D], [(x_hi[:, c, :], x_lo[:, c, :], x_hi[:, c, :], x_lo[:, c, :])])
                op.then_inc(front_full, 1)

            def score(i, k):
                c, g = k // 2, k % 2
                b = front_slot(i, f"SC{k}")
                at = (slice(None), slice(HG * g, HG * g + HG), slice(c * P, (c + 1) * P))
                xs = slice(c * P, (c + 1) * P)
                product(b[:].rearrange("p (a b) -> p a b", b=P),
                        [(xt_hi[:, xs], xt_lo[:, xs], qz_hi[at], qz_lo[at])]).then_inc(front_full, 1)

            def weighted(i, k):
                c, g = k // 2, k % 2
                b = front_slot(i, f"U{k}")
                at = (slice(None), slice(HG * g, HG * g + HG), slice(c * P, (c + 1) * P))
                pe.wait_ge(masked, i * GROUPS + k + 1)
                pairs = [(x_hi[:, c, :], x_lo[:, c, :], sc_hi[:, k % 4], sc_lo[:, k % 4])]
                if c:
                    if k == 2:
                        pe.wait_ge(state_split, i + 1)
                    pairs.append((st_hi[:, c - 1, :], st_lo[:, c - 1, :], qz_hi[at], qz_lo[at]))
                product(b[:].rearrange("p (a b) -> p a b", b=P), pairs).then_inc(front_full, 1)

            def y_product(n):
                b = back_slot(n, "Y")
                pe.wait_ge(front_free, n * NF)
                product(b[:], [(p_hi[:, h, :], p_lo[:, h, :], ut_hi[:, h, :], ut_lo[:, h, :]) for h in range(H)]).then_inc(full["Y"], 1)

            def t2(n):
                b = back_slot(n, "T2")
                pe.wait_ge(free["Y"], n)
                transposes(b, lambda c: vt[:, c * P:(c + 1) * P]).then_inc(full["T2"], 1)

            def t3(n):
                b = back_slot(n, "T3")
                pe.wait_ge(free["T2"], n)
                transposes(b, lambda c: z0[:, c, :]).then_inc(full["T3"], 1)

            def mlp_in(n):
                pe.wait_ge(free["T3"], n)
                for j, name in enumerate(("W1a", "W1b")):
                    b = back_slot(n, name)
                    pe.matmul(b[:], w1_sb[:, j * P:(j + 1) * P], zt[:], start=True, stop=True).then_inc(full[name], 1)

            def mlp_down(n):
                b = back_slot(n, "W2")
                pe.wait_ge(free["W1b"], n)
                pe.matmul(b[:], w2_sb[:, 0, :], m1[:, 0, :], start=True, stop=False)
                pe.matmul(b[:], w2_sb[:, 1, :], m1[:, 1, :], start=False, stop=True).then_inc(full["W2"], 1)

            def project(n):
                b = back_slot(n, "WP")
                pe.wait_ge(free["W2"], n)
                for c in range(C):
                    op = pe.matmul(b[:, c * D:(c + 1) * D], z2t[:, c * P:(c + 1) * P], wp_sb[:], start=True, stop=True)
                op.then_inc(full["WP"], 1)

            def t4(n):
                b = back_slot(n, "T4")
                pe.wait_ge(xf_ready, n)
                transposes(b, lambda c: xf[:, c, :]).then_inc(full["T4"], 1)

            def gate(n):
                b = back_slot(n, "G")
                pe.wait_ge(free["T4"], n)
                for c in range(C):
                    op = pe.matmul(b[:, c * E:(c + 1) * E], xft[:, c * P:(c + 1) * P], gate_sb[:], start=True, stop=True)
                op.then_inc(full["G"], 1)

            def shared_in(n):
                for name, w in (("S1", sw1_sb), ("S3", sw3_sb)):
                    b = back_slot(n, name)
                    pe.matmul(b[:], w[:], xft[:], start=True, stop=True).then_inc(full[name], 1)

            def counts(n):
                b = back_slot(n, "C")
                pe.wait_ge(either_made, n)
                pe.wait_ge(seen_made, n)
                pe.matmul(b[:, 0:C * E], upper[:], either[:], start=True, stop=False)
                for c in range(C):
                    for before in range(c):
                        pe.matmul(b[:, c * E:(c + 1) * E], ones[:], either[:, before, :], start=False, stop=False)
                op = pe.matmul(b[:, 0:C * E], ones[:], seen[:].unsqueeze(1).broadcast_to([P, C, E]), start=False, stop=True)
                op.then_inc(full["C"], 1)

            def shared_out(n):
                b = back_slot(n, "SW2")
                pe.wait_ge(free["S3"], n + 1)
                for c in range(C):
                    op = pe.matmul(b[:, c * D:(c + 1) * D], hs[:, c * P:(c + 1) * P], sw2_sb[:], start=True, stop=True)
                op.then_inc(full["SW2"], 1)

            def batch(i, behind):
                t1(i)
                if behind:
                    y_product(i)
                pe.wait_ge(front_free, i * NF + 1)
                for h in range(H):
                    if h == 3:
                        if FRONT_BANKS != 5:
                            raise ValueError("the bank of T1 is that of Q4")
                        if behind:
                            t2(i)
                    if h == 4:
                        pe.wait_ge(xt_ready, i + 1)
                    qz(i, h)
                pe.wait_ge(front_free, i * NF + FRONT.index("Q3") + 1)
                score(i, 0)
                outer(i)
                pe.wait_ge(front_free, i * NF + FRONT.index("Q7") + 1)
                score(i, 1)
                if behind:
                    t3(i)
                for k in range(2, GROUPS):
                    score(i, k)
                    if behind:
                        if k == 2:
                            mlp_in(i)
                        if k == 3:
                            mlp_down(i)
                        if k == 4:
                            project(i)
                        if k == 7:
                            t4(i)
                    weighted(i, k - 2)
                if behind:
                    gate(i)
                    shared_in(i)
                weighted(i, GROUPS - 2)
                weighted(i, GROUPS - 1)
                if behind:
                    counts(i)
                    shared_out(i)

            pe.wait_ge(const_made, 6)
            pe.wait_ge(q_lo_made, 1)
            batch(0, False)
            pe.wait_ge(w_small, 16 * SMALL)
            pe.wait_ge(p_lo_made, 1)
            with pe.Fori(1, NB) as i:
                batch(i, True)
            y_product(NB)
            t2(NB)
            t3(NB)
            mlp_in(NB)
            mlp_down(NB)
            project(NB)
            t4(NB)
            gate(NB)
            shared_in(NB)
            counts(NB)
            shared_out(NB)

            def rows_in(q, k):
                pe.wait_ge(rows_landed[k], q * (16 // PLACES) - k * (16 // PLACES) + 16)
                wait(pe, rows_t_ready, q - 1)
                for m in range(4):
                    op = pe.transpose(banks[k % 2][:, m * P:(m + 1) * P],
                                      rows[k][:, m // 2, (m % 2) * D:(m % 2 + 1) * D], identity[:])
                op.then_inc(rows_t_full, 1)

            def gate_up(q, k):
                pe.wait_ge(rows_t_ready, q + 1)
                pe.wait_ge(w13_landed[k], q * (16 // PLACES) - k * (16 // PLACES) + 16)
                wait(pe, hidden_ready, q - (PLACES - 1))
                for e in range(2):
                    op = pe.matmul(banks[2 + k][:, e * 2 * P:(e + 1) * 2 * P], w13[k][:, e, :],
                                   rows_t[k % 2][:, 2 * e:2 * e + 2, :], start=True, stop=True)
                op.then_inc(gu_full, 1)

            def down(q, k):
                pe.wait_ge(hidden_ready, q + 1)
                pe.wait_ge(w2_landed[k], q * (16 // PLACES) - k * (16 // PLACES) + 16)
                wait(pe, y_ready, q - 1)
                for m in range(4):
                    op = pe.matmul(banks[6 + k % 2][:, m * D:(m + 1) * D], hidden[k % 2][EH:P, m * P:(m + 1) * P],
                                   w2e[k][EH:P, m // 2, :], start=True, stop=True)
                op.then_inc(y_full, 1)

            def expert_step(p, k):
                if not (isinstance(p, int) and p + 3 >= PAIRS):
                    rows_in(p + 3, (k + 3) % PLACES)
                if not (isinstance(p, int) and p + 2 >= PAIRS):
                    gate_up(p + 2, (k + 2) % PLACES)
                down(p, k)

            pe.wait_ge(free["SW2"], NB + 1)
            for q in range(3):
                rows_in(q, q)
            gate_up(0, 0)
            gate_up(1, 1)
            for p in range(PLACES):
                expert_step(p, p)
            with pe.Fori(1, PAIRS // PLACES - 1) as g:
                for k in range(PLACES):
                    expert_step(g * PLACES + k, k)
            for k in range(PLACES):
                expert_step(PAIRS - PLACES + k, k)


def kernel(**inputs):
    import numpy as np
    import concourse.bacc as bacc
    from concourse.bass_utils import run_bass_kernel_spmd

    a = {k: np.asarray(v) for k, v in inputs.items()}
    nb, s = a["x"].shape
    d = a["L0_tok_W"].shape[0]
    e, _, eh = a["L0_ffn_w1"].shape
    tiles = nb * s // P
    w13 = np.concatenate([a["L0_ffn_w1"], a["L0_ffn_w3"]], axis=2)
    laid = {
        "ids": a["x"].reshape(tiles, P).T,
        "embed": a["L0_tok_W"].T,
        "pT": a["L0_attn_P"].transpose(2, 0, 1),
        "qT": a["L0_attn_Q"].transpose(2, 0, 1),
        "gamma": a["L0_attn_gamma"].reshape(d, 1),
        "beta": a["L0_attn_beta"].reshape(d, 1),
        "w1T": a["L0_attn_W1"].T,
        "b1": a["L0_attn_b1"].reshape(2, d).T,
        "w2T": a["L0_attn_W2"].T.reshape(2, d, d).transpose(1, 0, 2),
        "b2": a["L0_attn_b2"].reshape(d, 1),
        "wpT": a["L0_attn_Wp"].T,
        "bp": a["L0_attn_bp"].reshape(1, d),
        "gateT": a["L0_ffn_gate_w"].T,
        "ew13": w13.reshape(e // 2, 2, d, 2 * eh).transpose(0, 2, 1, 3),
        "ew2": a["L0_ffn_w2"].reshape(e // 2, 2, eh, d).transpose(0, 2, 1, 3),
        "sw1": a["L0_ffn_sw1"],
        "sw3": a["L0_ffn_sw3"],
        "sw2": a["L0_ffn_sw2"],
    }
    nc = bacc.Bacc("TRN2", target_bir_lowering=False, num_devices=1)
    arrays, args = {}, []
    for name, v in laid.items():
        v = np.ascontiguousarray(v)
        arrays[f"in_{name}"] = v
        args.append(nc.dram_tensor(f"in_{name}", v.shape, mybir.dt.from_np(v.dtype), kind="ExternalInput").ap())
    args.append(nc.dram_tensor("out_0", (nb, s, d), F32, kind="ExternalOutput").ap())
    tower(nc, *args)
    r = run_bass_kernel_spmd(nc, [arrays], core_ids=[0])
    return r.results[0]["out_0"]
```

```python
from contextlib import ExitStack

import concourse.bass as bass
from concourse import mybir
from concourse.alu_op_type import AluOpType as ALU

ACT = mybir.ActivationFunctionType
AXES = mybir.AxisListType
F32 = mybir.dt.float32
F32R = mybir.dt.float32r
BF16 = mybir.dt.bfloat16
I32 = mybir.dt.int32
U32 = mybir.dt.uint32

P = 128

TOP_K = 2
CAP = 256
ROUTE_SCALE = 2.5
LN_EPS = 1e-5
PADDING_IDX = 0
DROPPED = 1 << 20

HEADS = 8
GROUPS = 8

FRONT = [f"Q{_h}" for _h in range(HEADS)] + ["SC0", "X", "SC1", "SC2"]
for _k in range(GROUPS - 3):
    FRONT += [f"SC{_k + 3}", f"U{_k}"]
FRONT += ["U5", "U6", "T1", "U7"]
NF = len(FRONT)
AFTER_T1 = FRONT[FRONT.index("T1") + 1:]
FRONT_BANKS = 5


def front_bank(name):
    return FRONT.index(name) % FRONT_BANKS


def front_count(i, name):
    if name == "T1":
        return 1 if isinstance(i, int) and i == 0 else (i - 1) * NF + (FRONT.index("T1") + 2)
    return i * NF + (FRONT.index(name) + 2 - (name in AFTER_T1 and isinstance(i, int) and i == LAST_BATCH))


def front_before(i, name):
    if name == "T1":
        i = i - 1
    at = FRONT.index(name)
    if at >= FRONT_BANKS:
        return i * NF + (at - FRONT_BANKS + 2)
    last = max(k for k in range(NF) if k % FRONT_BANKS == at)
    return i * NF + (last + 2 - NF)


LAST_BATCH = 7

BACK = {
    "Y": (0, "W1b", -1), "T4": (0, "Y", 1), "W1b": (0, "T4", -1),
    "T2": (1, "WP", -1), "T3": (1, "T2", 0), "C": (1, "T3", 1), "WP": (1, "C", -1),
    "G": (2, "W2", 0), "W1a": (2, "G", -1), "W2": (2, "W1a", 0),
}
LAST_HALF = {"T4": 0, "G": 1, "C": 2}
LAST_BEFORE = {"T4": ("W1b", 0), "C": ("WP", 0)}


def back_bank(name):
    return FRONT_BANKS + BACK[name][0]


def tower(nc, ids, embed, pT, qT, gamma, beta, w1T, b1, w2T, b2, wpT, bp, gateT, ew13, ew2, sw1, sw3, sw2, out):
    NB, S, D = out.shape
    C = S // P
    TILES = NB * C
    H = qT.shape[1]
    E = gateT.shape[1]
    EH = ew2.shape[1]
    PAIRS = E // 2
    SLOTS = E * CAP
    HG = H // 2
    SCORE_SCALE = 1.0 / (H * float(D) ** 0.5)
    assert NB == LAST_BATCH + 1 and D == P and C == 4 and H == HEADS and H * C // HG == GROUPS and CAP == 2 * P and EH == P // 2

    out_v = out.rearrange("b (c p) d -> b p c d", p=P)
    xbuf = nc.dram_tensor("expert_rows_in", (SLOTS, D), F32, kind="Internal").ap()
    ybuf = nc.dram_tensor("expert_rows_out", (SLOTS, D), F32, kind="Internal").ap()
    xbuf_v = xbuf.rearrange("(q e p r) d -> q p e (r d)", e=2, p=P, r=2)
    ybuf_v = ybuf.rearrange("(q e p r) d -> q p e (r d)", e=2, p=P, r=2)
    ZW = H * D
    PLACES = 4
    xbuf_z = xbuf.rearrange("(z p r) d -> z p (r d)", p=P, r=ZW // D)
    NZ = SLOTS * D // (P * ZW)

    ctx = ExitStack()
    with ctx:
        def sb(name, shape, dt=F32):
            return ctx.enter_context(nc.sbuf_tensor(name, shape, dt))

        def sem(name):
            return ctx.enter_context(nc.semaphore(name))

        identity = sb("identity", [P, P])
        upper = sb("upper", [P, P], BF16)
        ones = sb("ones", [P, P], BF16)
        expert_iota = sb("expert_iota", [P, E])
        minus_half = sb("minus_half", [P, C])
        ids_sb = sb("ids_sb", [P, TILES], I32)
        not_pad = sb("not_pad", [P, TILES])
        raw_q, raw_p = sb("raw_q", [P, H, D]), sb("raw_p", [P, H, D])
        zeros = raw_q
        q_hi, q_lo = sb("q_hi", [P, H, D], F32R), sb("q_lo", [P, H, D], F32R)
        p_hi, p_lo = sb("p_hi", [P, H, D], F32R), sb("p_lo", [P, H, D], F32R)
        gamma_sb, beta_sb, b2_sb = sb("gamma_sb", [P, 1]), sb("beta_sb", [P, 1]), sb("b2_sb", [P, 1])
        b1_sb = sb("b1_sb", [P, 2])
        bp_sb = sb("bp_sb", [P, D])
        w1_sb, w2_sb, wp_sb = sb("w1_sb", [P, 2 * D]), sb("w2_sb", [P, 2, D]), sb("wp_sb", [P, D])
        gate_sb = sb("gate_sb", [P, E])
        sw1_sb, sw3_sb, sw2_sb = sb("sw1_sb", [P, D]), sb("sw3_sb", [P, D]), sb("sw2_sb", [P, D])

        stream = sb("stream", [P, TILES, D])
        pair_slot = sb("pair_slot", [P, NB, TOP_K * C], I32)
        pair_weight = sb("pair_weight", [P, NB, TOP_K * C])

        ids_now = sb("ids_now", [P, C], I32)
        gathered = sb("gathered", [P, C, D])
        emb = sb("emb", [P, C, D])
        stats1, mv1 = sb("stats1", [P, C, 6]), sb("mv1", [P, C, 2])
        var1, rstd1, shift1 = sb("var1", [P, C]), sb("rstd1", [P, C]), sb("shift1", [P, C])
        xn = sb("xn", [P, C, D])
        x_hi, x_lo = sb("x_hi", [P, C, D], F32R), sb("x_lo", [P, C, D], F32R)
        xt_hi, xt_lo = sb("xt_hi", [P, S], F32R), sb("xt_lo", [P, S], F32R)
        xt = sb("xt", [P, S])
        state = sb("state", [P, C - 1, D])
        st_hi, st_lo = sb("st_hi", [P, C - 1, D], F32R), sb("st_lo", [P, C - 1, D], F32R)
        vt = sb("vt", [P, S])
        stats2, mv2 = sb("stats2", [P, C, 6]), sb("mv2", [P, C, 2])
        var2, rstd2, shift2 = sb("var2", [P, C]), sb("rstd2", [P, C]), sb("shift2", [P, C])
        z0 = sb("z0", [P, C, D])
        zt = sb("zt", [P, S])
        m1 = sb("m1", [P, 2, S])
        z2t = sb("z2t", [P, S])
        stats3, mv3 = sb("stats3", [P, C, 6]), sb("mv3", [P, C, 2])
        var3, rstd3, shift3 = sb("var3", [P, C]), sb("rstd3", [P, C]), sb("shift3", [P, C])
        xf, xf_send = sb("xf", [P, C, D]), sb("xf_send", [P, C, D])
        xft, xft_all = sb("xft", [P, S]), sb("xft_all", [P, NB, S])
        scores = sb("scores", [P, C, E])
        top8, index8 = sb("top8", [P, C, 8]), sb("index8", [P, C, 8], U32)
        index2 = sb("index2", [P, TOP_K, C])
        chosen = sb("chosen", [P, TOP_K, C, E])
        chosen_pos = sb("chosen_pos", [P, TOP_K, C, E])
        either = sb("either", [P, C, E], BF16)
        seen, seen_new = sb("seen", [P, E], BF16), sb("seen_new", [P, E])
        pos = sb("pos", [P, TOP_K, C])
        kept = sb("kept", [P, TOP_K, C])
        pos_in = sb("pos_in", [P, TOP_K, C])
        slot_f = sb("slot_f", [P, TOP_K, C])
        slot_drop = sb("slot_drop", [P, TOP_K, C])
        slot_out = sb("slot_out", [P, TOP_K * C], I32)
        top_sum, top_inv = sb("top_sum", [P, C]), sb("top_inv", [P, C])
        weight = sb("weight", [P, TOP_K, C])
        silu = [xt, vt]
        hidden = [zt, z2t]
        shared_silu, shared_hidden = xn, z0
        slot_now = [sb(f"slot_now{k}", [P, TOP_K * C], I32) for k in range(2)]
        y_got = [raw_q, raw_p]

        with ExitStack() as attention:
            def shared_sb(name, shape):
                return attention.enter_context(nc.sbuf_tensor(name, shape, F32R))

            qz_hi, qz_lo = shared_sb("qz_hi", [P, H, S]), shared_sb("qz_lo", [P, H, S])
            sc_hi, sc_lo = shared_sb("sc_hi", [P, 4, HG, P]), shared_sb("sc_lo", [P, 4, HG, P])
            ut_hi, ut_lo = shared_sb("ut_hi", [P, H, S]), shared_sb("ut_lo", [P, H, S])
            w1_hi, w1_lo = shared_sb("w1_hi", [P, 2 * D]), shared_sb("w1_lo", [P, 2 * D])
            w2_hi, w2_lo = shared_sb("w2_hi", [P, 2, D]), shared_sb("w2_lo", [P, 2, D])
            zt_hi, zt_lo = shared_sb("zt_hi", [P, S]), shared_sb("zt_lo", [P, S])
            m1_hi, m1_lo = shared_sb("m1_hi", [P, 2, S]), shared_sb("m1_lo", [P, 2, S])
        w13_all, w2_all = sb("w13_all", [P, PAIRS, 2, P]), sb("w2_all", [P, PAIRS, 2, D])
        rows = [sb(f"rows{k}", [P, 2, 2 * D]) for k in range(PLACES)]
        rows_t_hi = [xt_hi[:], x_hi[:].rearrange("p c d -> p (c d)")] + [sb(f"rows_t_hi{k}", [P, 4 * P], F32R)[:] for k in (2, 3)]
        rows_t_lo = [xt_lo[:], x_lo[:].rearrange("p c d -> p (c d)")] + [sb(f"rows_t_lo{k}", [P, 4 * P], F32R)[:] for k in (2, 3)]
        y_sb = [sb(f"y_sb{k}", [P, 2, 2 * D]) for k in range(PLACES)]
        w13_hi = [sb(f"w13_hi{k}", [P, 2, P], F32R) for k in range(PLACES)]
        w13_lo = [sb(f"w13_lo{k}", [P, 2, P], F32R) for k in range(PLACES)]

        banks = [ctx.enter_context(nc.psum_tensor(f"bank{k}", [P, S], F32)) for k in range(8)]

        wait_carried = sem("wait_carried")
        w_q = sem("w_q_landed")
        w_p = sem("w_p_landed")
        w_bp = sem("bp_landed")
        w_small = sem("small_weights_landed")
        w_ids = sem("ids_landed")
        const_made = sem("constants_made")
        const_step = sem("constant_begun")
        q_hi_made, q_lo_made = sem("q_hi_made"), sem("q_lo_made")
        p_hi_made, p_lo_made = sem("p_hi_made"), sem("p_lo_made")
        pad_made = sem("pad_mask_made")
        zero_made = sem("zeros_made")
        zero_filled = sem("expert_rows_zeroed")
        ids_copied = sem("ids_copied")
        emb_landed = sem("embeddings_landed")
        emb_masked = sem("embeddings_masked")
        stream_begun = sem("stream_begun")
        ln1_stats, ln1_mean, ln1_var = sem("ln1_stats"), sem("ln1_mean"), sem("ln1_var")
        ln1_rstd, ln1_shift, xn_ready = sem("ln1_rstd"), sem("ln1_shift"), sem("xn_ready")
        x_hi_ready, x_split = sem("x_hi_ready"), sem("x_split")
        xt_ready = sem("xt_ready")
        front_full, front_hi, front_free = sem("front_full"), sem("front_hi"), sem("front_free")
        state_step, state_hi, state_split = sem("state_step"), sem("state_hi"), sem("state_split")
        masked = sem("scores_masked")
        full = {n: sem(f"{n}_full") for n in BACK}
        free = {n: sem(f"{n}_free") for n in BACK}
        ln2_stats, ln2_mean, ln2_var = sem("ln2_stats"), sem("ln2_mean"), sem("ln2_var")
        ln2_rstd, ln2_shift = sem("ln2_rstd"), sem("ln2_shift")
        ln3_stats, ln3_mean, ln3_var = sem("ln3_stats"), sem("ln3_mean"), sem("ln3_var")
        ln3_rstd, ln3_shift, xf_ready = sem("ln3_rstd"), sem("ln3_shift"), sem("xf_ready")
        mlp_hi_made, mlp_lo_made = sem("mlp_weights_hi_made"), sem("mlp_weights_lo_made")
        zt_split, m1_split = sem("zt_split"), sem("m1_split")
        top_found, index_found, index_float = sem("top_found"), sem("index_found"), sem("index_float")
        chosen_made, either_made = sem("chosen_made"), sem("either_made")
        seen_sum, seen_made = sem("seen_sum"), sem("seen_made")
        pos_made, kept_made, slot_made = sem("pos_made"), sem("kept_made"), sem("slot_made")
        slots_kept = sem("slots_kept")
        slots_ready, send_ready, rows_sent = sem("slots_ready"), sem("send_ready"), sem("rows_sent")
        weight_step, weight_ready = sem("weight_step"), sem("weight_ready")
        xft_ready = sem("xft_ready")
        rows_landed = [sem(f"rows_landed{k}") for k in range(PLACES)]
        expert_weights = sem("expert_weights_landed")
        w13_hi_ready, w13_split, rows_t_hi_ready = sem("w13_hi_ready"), sem("w13_split"), sem("rows_t_hi_ready")
        rows_t_full, rows_t_ready = sem("rows_t_full"), sem("rows_t_ready")
        gu_full, silu_ready, hidden_ready = sem("gu_full"), sem("silu_ready"), sem("hidden_ready")
        y_full, y_ready = sem("y_full"), sem("y_ready")
        y_stored = [sem(f"y_stored{k}") for k in range(PLACES)]
        s1_full, s3_full, s2_full = sem("shared1_full"), sem("shared3_full"), sem("shared2_full")
        shared_silu_ready, shared_hidden_ready, shared_added = sem("shared_silu_ready"), sem("shared_hidden_ready"), sem("shared_added")
        slot_copied = sem("slot_copied")
        y_landed = [[sem(f"y_landed{k}_{c}") for c in range(TOP_K * C)] for k in range(2)]
        pair_added, tiles_done = sem("pair_added"), sem("tiles_done")
        out_stored = sem("out_stored")

        SMALL = 11
        block = ctx.enter_context(nc.Block())

        def wait(eng, s, value):
            if not (isinstance(value, int) and value <= 0):
                eng.wait_ge(s, value)

        def carried(eng):
            eng.sem_inc(wait_carried, 1)

        def tiles_of(half):
            return range(C) if half is None else range(half * C // 2, (half + 1) * C // 2)

        def back_place(name, half):
            return banks[LAST_HALF[name]] if half == 1 else banks[back_bank(name)]

        def upto(n, half):
            return n if half is None else n + half

        def tiles_upto(n, half):
            return n * C if half is None else (n - 1) * C + (half + 1) * C // 2

        def tile_slice(i):
            return bass.ds(i * C, C)

        @block.sync
        def _(sp):
            sp.dma_start(ids_sb[:], ids).then_inc(w_ids, 16)
            sp.dma_start(raw_q[:], qT).then_inc(w_q, 16)
            sp.dma_start(bp_sb[:], bp.broadcast_to([P, D])).then_inc(w_bp, 16)
            sp.dma_start(raw_p[:], pT).then_inc(w_p, 16)
            for dst, src in ((gamma_sb[:], gamma), (beta_sb[:], beta), (b1_sb[:], b1), (b2_sb[:], b2),
                             (w1_sb[:], w1T), (w2_sb[:], w2T), (wp_sb[:], wpT), (gate_sb[:], gateT),
                             (sw1_sb[:], sw1), (sw3_sb[:], sw3), (sw2_sb[:], sw2)):
                sp.dma_start(dst, src).then_inc(w_small, 16)
            sp.wait_ge(zero_made, 1)
            sp.wait_ge(emb_landed, 16 * C * 3)
            with sp.Fori(0, NZ) as z:
                sp.dma_start(xbuf_z[bass.ds(z, 1)].rearrange("z p n -> p (z n)"), zeros[:].rearrange("p h d -> p (h d)")).then_inc(zero_filled, 16)

            sp.wait_ge(full["Y"], NB)
            sp.wait_ge(rows_sent, 16 * TOP_K * C * (NB - 2))
            sp.dma_start(w13_all[:], ew13.rearrange("q p e f -> p q e f")).then_inc(expert_weights, 16)
            sp.dma_start(w2_all[0:EH], ew2.rearrange("q f e d -> f q e d")).then_inc(expert_weights, 16)

            def load_rows(q, k):
                wait(sp, rows_t_full, q - (PLACES - 1))
                sp.dma_start(rows[k][:], xbuf_v[bass.ds(q, 1)].rearrange("q p e n -> p (q e) n")).then_inc(rows_landed[k], 16)

            sp.wait_ge(rows_sent, 16 * TILES * TOP_K)
            for k in range(PLACES):
                load_rows(k, k)
            with sp.Fori(1, PAIRS // PLACES) as g:
                for k in range(PLACES):
                    load_rows(g * PLACES + k, k)

            with sp.Fori(0, NB) as i:
                sp.wait_ge(tiles_done, i + 1)
                sp.dma_start(out_v[bass.ds(i, 1)].rearrange("b p c d -> p (b c) d"), stream[:, tile_slice(i), :]).then_inc(out_stored, 16)
            sp.wait_ge(out_stored, 16 * NB)

        @block.gpsimd
        def _(pool):
            pool.memset(identity[:], 0.0).then_inc(const_step, 1)
            pool.memset(upper[:], 1.0).then_inc(const_step, 1)
            pool.memset(ones[:], 1.0).then_inc(const_made, 1)
            pool.memset(minus_half[:], -0.5).then_inc(const_made, 1)
            pool.memset(seen[:], 0.0).then_inc(const_made, 1)
            pool.iota(expert_iota[:], pattern=[[1, E]], base=0, channel_multiplier=0,
                      allow_small_or_imprecise_dtypes=True).then_inc(const_made, 1)
            pool.wait_ge(const_step, 2)
            pool.affine_select(out=identity[:], in_=identity[:], compare_op=ALU.not_equal, fill=1.0,
                               base=0, pattern=[[-1, P]], channel_multiplier=1).then_inc(const_made, 1)
            pool.affine_select(out=upper[:], in_=upper[:], compare_op=ALU.is_gt, fill=0.0,
                               base=0, pattern=[[1, P]], channel_multiplier=-1).then_inc(const_made, 1)

            def gather(i, c):
                if c == 0:
                    wait(pool, emb_landed, i * (16 * C))
                    pool.tensor_copy(ids_now[:], ids_sb[:, tile_slice(i)]).then_inc(ids_copied, 1)
                    pool.wait_ge(ids_copied, i + 1)
                    wait(pool, emb_masked, i * C)
                    carried(pool)
                pool.indirect_dma_start(
                    out=gathered[:, c, :], out_offset=None, in_=embed,
                    in_offset=bass.IndirectOffsetOnAxis(ap=ids_now[:, c:c + 1], axis=0)).then_inc(emb_landed, 16)

            def inverse_deviation(out_ap, var, var_ready, ready, n):
                pool.wait_ge(var_ready, n)
                pool.tensor_tensor(out_ap[:], var[:], minus_half[:], ALU.pow).then_inc(ready, 1)

            def begin_stream(i):
                pool.wait_ge(emb_masked, i * C + C)
                pool.tensor_tensor(stream[:, tile_slice(i), :], emb[:],
                                   bp_sb[:].unsqueeze(1).broadcast_to([P, C, D]), ALU.add).then_inc(stream_begun, 1)

            def x_low(i):
                pool.wait_ge(x_hi_ready, i + 1)
                pool.tensor_tensor(x_lo[:], xn[:], x_hi[:].bitcast(F32), ALU.subtract).then_inc(x_split, 1)

            def state_low(i):
                pool.wait_ge(state_hi, i + 1)
                pool.tensor_tensor(st_lo[:], state[:], st_hi[:].bitcast(F32), ALU.subtract).then_inc(state_split, 1)

            def zt_low(n):
                pool.wait_ge(free["T3"], n)
                pool.tensor_tensor(zt_lo[:], zt[:], zt_hi[:].bitcast(F32), ALU.subtract).then_inc(zt_split, 1)

            def mask(i, k):
                pool.wait_ge(front_free, front_count(i, f"SC{k}"))
                carried(pool)
                pool.affine_select(out=sc_hi[:, k % 4], in_=sc_hi[:, k % 4].bitcast(F32), compare_op=ALU.is_ge,
                                   fill=0.0, base=0, pattern=[[0, HG], [1, P]], channel_multiplier=-1)
                pool.affine_select(out=sc_lo[:, k % 4], in_=sc_lo[:, k % 4].bitcast(F32), compare_op=ALU.is_ge,
                                   fill=0.0, base=0, pattern=[[0, HG], [1, P]], channel_multiplier=-1).then_inc(masked, 1)

            def dispatch(n, m, half=None):
                if m == 0 or half is not None:
                    pool.wait_ge(send_ready, upto(n, half))
                    pool.wait_ge(slots_ready, upto(n, half))
                    carried(pool)
                pool.indirect_dma_start(
                    out=xbuf, out_offset=bass.IndirectOffsetOnAxis(ap=slot_out[:, m:m + 1], axis=0),
                    in_=xf_send[:, m % C, :], in_offset=None,
                    bounds_check=SLOTS - 1, oob_is_err=False).then_inc(rows_sent, 16)

            def batch(i, more, behind, routed):
                if more:
                    gather(i + 1, 0)
                    gather(i + 1, 1)
                if behind:
                    inverse_deviation(rstd2, var2, ln2_var, ln2_rstd, i)
                if more:
                    gather(i + 1, 2)
                    gather(i + 1, 3)
                mask(i, 0)
                mask(i, 1)
                if behind:
                    zt_low(i)
                state_low(i)
                mask(i, 2)
                mask(i, 3)
                mask(i, 4)
                if more:
                    inverse_deviation(rstd1, var1, ln1_var, ln1_rstd, i + 2)
                mask(i, 5)
                mask(i, 6)
                mask(i, 7)
                if more:
                    begin_stream(i + 1)
                if routed:
                    dispatch(i - 1, 0)
                    dispatch(i - 1, 1)
                    dispatch(i - 1, 2)
                    dispatch(i - 1, 3)
                if behind:
                    inverse_deviation(rstd3, var3, ln3_var, ln3_rstd, i)
                if routed:
                    dispatch(i - 1, 4)
                    dispatch(i - 1, 5)
                    dispatch(i - 1, 6)
                    dispatch(i - 1, 7)
                if more:
                    x_low(i + 1)

            pool.wait_ge(w_ids, 16)
            for c in range(C):
                gather(0, c)
            inverse_deviation(rstd1, var1, ln1_var, ln1_rstd, 1)
            pool.wait_ge(w_bp, 16)
            begin_stream(0)
            x_low(0)
            batch(0, True, False, False)
            pool.wait_ge(q_lo_made, 1)
            pool.memset(zeros[:], 0.0).then_inc(zero_made, 1)
            batch(1, True, True, False)
            pool.wait_ge(zero_filled, 16 * NZ)
            batch(2, True, True, True)
            with pool.Fori(3, NB - 1) as i:
                batch(i, True, True, True)
            batch(NB - 1, False, True, True)
            inverse_deviation(rstd2, var2, ln2_var, ln2_rstd, NB)
            zt_low(NB)
            dispatch(NB - 1, 0)
            dispatch(NB - 1, 2)
            dispatch(NB - 1, 1)
            inverse_deviation(rstd3, var3, ln3_var, ln3_rstd, NB)
            dispatch(NB - 1, 3)
            dispatch(NB - 1, 4)
            dispatch(NB - 1, 5)
            dispatch(NB - 1, 7)
            dispatch(NB - 1, 6)
            dispatch(NB, 0, 0)
            dispatch(NB, 1, 0)
            dispatch(NB, 4, 0)
            dispatch(NB, 5, 0)
            dispatch(NB, 2, 1)
            dispatch(NB, 3, 1)
            dispatch(NB, 6, 1)
            dispatch(NB, 7, 1)

            def w13_low(q, k):
                pool.wait_ge(w13_hi_ready, q + 1)
                pool.tensor_tensor(w13_lo[k][:], w13_all[:, bass.ds(q, 1)].rearrange("p q e f -> p (q e) f"),
                                   w13_hi[k][:].bitcast(F32), ALU.subtract).then_inc(w13_split, 1)

            for k in range(PLACES):
                w13_low(k, k)
            with pool.Fori(1, PAIRS // PLACES) as g:
                for k in range(PLACES):
                    w13_low(g * PLACES + k, k)

            def copy_slots(i, k):
                wait(pool, tiles_done, i - 1)
                pool.tensor_copy(slot_now[k][:], pair_slot[:, bass.ds(i, 1), :].rearrange("p b m -> p (b m)")).then_inc(slot_copied, 1)

            def fetch(i, k, more=True):
                pool.wait_ge(slot_copied, i + 1)
                carried(pool)
                for m in range(TOP_K * C):
                    if m == 6 and more:
                        copy_slots(i + 1, 1 - k)
                    pool.indirect_dma_start(
                        out=y_got[k][:, m, :], out_offset=None, in_=ybuf,
                        in_offset=bass.IndirectOffsetOnAxis(ap=slot_now[k][:, m:m + 1], axis=0)).then_inc(y_landed[k][m], 16)

            pool.wait_ge(slots_kept, NB)
            copy_slots(0, 0)
            for k in range(PLACES):
                pool.wait_ge(y_stored[k], 16 * PAIRS // PLACES)
            fetch(0, 0)
            fetch(1, 1)
            with pool.Fori(1, NB // 2 - 1) as g:
                for k in range(2):
                    fetch(g * 2 + k, k)
            fetch(NB - 2, 0)
            fetch(NB - 1, 1, more=False)

        @block.scalar
        def _(act):
            act.preload_act_table(ACT.Sigmoid)

            def embed_in(i):
                act.wait_ge(emb_landed, i * (16 * C) + 16 * C)
                wait(act, xn_ready, i * C)
                wait(act, stream_begun, i)
                for c in range(C):
                    act.activation(emb[:, c, :], gathered[:, c, :], ACT.Copy,
                                   scale=not_pad[:, bass.ds(i * C + c, 1)]).then_inc(emb_masked, 1)

            def normalise(i):
                act.wait_ge(ln1_shift, i + 1)
                wait(act, x_split, i)
                for c in range(C):
                    act.activation(xn[:, c, :], emb[:, c, :], ACT.Identity, scale=rstd1[:, c:c + 1],
                                   bias=shift1[:, c:c + 1]).then_inc(xn_ready, 1)

            def x_high(i):
                if not isinstance(i, int) or i > 0:
                    act.wait_ge(front_full, front_count(i - 1, "U7"))
                act.wait_ge(xn_ready, i * C + C)
                act.copy(x_hi[:], xn[:]).then_inc(x_hi_ready, 1)

            def leading(i, name, dst, scale=1.0):
                b = banks[front_bank(name)]
                act.wait_ge(front_full, front_count(i, name))
                src = b[:] if len(dst.shape) == 2 else b[:].rearrange("p (a b) -> p a b", b=P)
                act.activation(dst, src, ACT.Copy, scale=scale).then_inc(front_hi, 1)

            def keep_xt(i):
                wait(act, free["Y"], i)
                act.copy(xt[:], banks[front_bank("T1")][:]).then_inc(xt_ready, 1)

            def ln_mid_apply(n):
                act.wait_ge(ln2_shift, n)
                for c in range(C):
                    op = act.activation(z0[:, c, :], banks[back_bank("T2")][:, c * D:(c + 1) * D], ACT.Identity,
                                        scale=rstd2[:, c:c + 1], bias=shift2[:, c:c + 1])
                op.then_inc(free["T2"], 1)

            def gamma_beta(n):
                act.wait_ge(full["T3"], n)
                act.activation(zt[:], banks[back_bank("T3")][:], ACT.Identity, bias=beta_sb[:], scale=gamma_sb[:])
                act.activation(zt_hi[:], banks[back_bank("T3")][:], ACT.Identity, bias=beta_sb[:], scale=gamma_sb[:]).then_inc(free["T3"], 1)

            def relu(n, j):
                name = "W1a" if j == 0 else "W1b"
                act.wait_ge(full[name], n)
                wait(act, m1_split, n * 2 - 2)
                act.activation(m1[:, j, :], banks[back_bank(name)][:], ACT.Relu, bias=b1_sb[:, j:j + 1])
                act.activation(m1_hi[:, j, :], banks[back_bank(name)][:], ACT.Relu, bias=b1_sb[:, j:j + 1]).then_inc(free[name], 1)

            def ln_last_apply(n, i, half=None):
                act.wait_ge(ln3_shift, n)
                wait(act, send_ready, n - 1)
                for c in tiles_of(half):
                    op = act.activation(xf[:, c, :], stream[:, bass.ds(i * C + c, 1), :].rearrange("p a d -> p (a d)"),
                                        ACT.Identity, scale=rstd3[:, c:c + 1], bias=shift3[:, c:c + 1])
                op.then_inc(xf_ready, 1)

            def send_copy(n, half=None):
                act.wait_ge(xf_ready, upto(n, half))
                wait(act, rows_sent, (n - 1) * (16 * TOP_K * C))
                t = tiles_of(half)
                act.copy(xf_send[:, t[0]:t[-1] + 1], xf[:, t[0]:t[-1] + 1]).then_inc(send_ready, 1)

            def copy_xft(n, half=None):
                act.wait_ge(full["T4"], upto(n, half))
                t = tiles_of(half)
                at = slice(t[0] * P, (t[-1] + 1) * P)
                act.activation(xft[:, at], back_place("T4", half)[:, at], ACT.Copy).then_inc(xft_ready, 1)

            def keep_xft(i, half=None):
                t = tiles_of(half)
                at = slice(t[0] * P, (t[-1] + 1) * P)
                act.activation(xft_all[:, bass.ds(i, 1), at].rearrange("p b s -> p (b s)"), back_place("T4", half)[:, at],
                               ACT.Copy).then_inc(free["T4"], 1)

            def gate_sigmoid(n, half=None):
                act.wait_ge(full["G"], upto(n, half))
                t = tiles_of(half)
                act.activation(scores[:, t[0]:t[-1] + 1],
                               back_place("G", half)[:, t[0] * E:(t[-1] + 1) * E].rearrange("p (c e) -> p c e", e=E),
                               ACT.Sigmoid).then_inc(free["G"], 1)

            def state_high(i):
                act.wait_ge(state_step, i * 3 + 3)
                act.copy(st_hi[:], state[:]).then_inc(state_hi, 1)

            def weights_high():
                act.wait_ge(w_p, 16)
                act.copy(p_hi[:], raw_p[:]).then_inc(p_hi_made, 1)
                act.wait_ge(w_small, 16 * SMALL)
                act.copy(w1_hi[:], w1_sb[:]).then_inc(mlp_hi_made, 1)
                act.copy(w2_hi[:], w2_sb[:]).then_inc(mlp_hi_made, 1)

            def batch(i, more, behind, routed):
                for name in FRONT:
                    k = int(name[-1]) if name != "X" else 0
                    if name.startswith("Q"):
                        leading(i, name, qz_hi[:, k, :], SCORE_SCALE)
                    elif name.startswith("SC"):
                        leading(i, name, sc_hi[:, k % 4])
                    elif name.startswith("U"):
                        c, g = k // 2, k % 2
                        leading(i, name, ut_hi[:, HG * g:HG * g + HG, c * P:(c + 1) * P])
                    elif name == "T1" and more:
                        leading(i + 1, "T1", xt_hi[:])
                    if name == "Q0":
                        keep_xt(i)
                    if name == "Q3" and routed:
                        copy_xft(i - 1)
                    if name == "Q5" and routed:
                        keep_xft(i - 2)
                    if name == "Q6" and routed:
                        gate_sigmoid(i - 1)
                    if name == "X" and behind:
                        ln_mid_apply(i)
                    if name == "SC2" and behind:
                        gamma_beta(i)
                    if name == "SC3":
                        state_high(i)
                    if name == "U1":
                        if more:
                            embed_in(i + 1)
                        if not behind:
                            weights_high()
                    if name == "SC5" and behind:
                        relu(i, 0)
                    if name == "U2" and behind:
                        relu(i, 1)
                    if name == "SC7" and routed:
                        send_copy(i - 1)
                    if name == "U4" and more:
                        normalise(i + 1)
                    if name == "T1" and more:
                        x_high(i + 1)
                    if name == "U7" and behind:
                        ln_last_apply(i, i - 1)

            act.wait_ge(w_q, 16)
            act.copy(q_hi[:], raw_q[:]).then_inc(q_hi_made, 1)
            act.wait_ge(pad_made, 1)
            embed_in(0)
            normalise(0)
            leading(0, "T1", xt_hi[:])
            x_high(0)
            batch(0, True, False, False)
            batch(1, True, True, False)
            batch(2, True, True, True)
            with act.Fori(3, NB - 1) as i:
                batch(i, True, True, True)
            batch(NB - 1, False, True, True)
            copy_xft(NB - 1)
            keep_xft(NB - 2)
            gate_sigmoid(NB - 1)
            ln_mid_apply(NB)
            send_copy(NB - 1)
            gamma_beta(NB)
            relu(NB, 0)
            relu(NB, 1)
            ln_last_apply(NB, NB - 1, 0)
            ln_last_apply(NB, NB - 1, 1)
            copy_xft(NB, 0)
            copy_xft(NB, 1)
            gate_sigmoid(NB, 0)
            gate_sigmoid(NB, 1)
            send_copy(NB, 0)
            send_copy(NB, 1)
            keep_xft(NB - 1, 0)
            keep_xft(NB - 1, 1)

            def rows_high(q, k):
                act.wait_ge(rows_t_full, q + 1)
                wait(act, gu_full, q - (PLACES - 1))
                act.copy(rows_t_hi[k], banks[k % 2][:]).then_inc(rows_t_hi_ready, 1)

            def silu_of(q, k):
                act.wait_ge(gu_full, q + 1)
                wait(act, hidden_ready, q - 1)
                act.activation(silu[k % 2][EH:P, :], banks[2 + k][0:EH, :], ACT.Silu).then_inc(silu_ready, 1)

            def y_out(q, k):
                act.wait_ge(y_full, q + 1)
                wait(act, y_stored[k], q * (16 // PLACES) - k * (16 // PLACES))
                act.activation(y_sb[k][:].rearrange("p e n -> p (e n)"), banks[6 + k % 2][:], ACT.Copy).then_inc(y_ready, 1)

            def y_store(q, k):
                act.wait_ge(y_ready, q + 1)
                act.dma_start(ybuf_v[bass.ds(q, 1)].rearrange("q p e n -> p (q e) n"), y_sb[k][:]).then_inc(y_stored[k], 16)

            def expert_step(p, k):
                if not (isinstance(p, int) and p + 4 >= PAIRS):
                    rows_high(p + 4, k)
                if not (isinstance(p, int) and p + 2 >= PAIRS):
                    silu_of(p + 2, (k + 2) % PLACES)
                y_out(p, k)
                if not (isinstance(p, int) and p == 0):
                    y_store(p - 1, (k - 1) % PLACES)

            for q in range(PLACES):
                rows_high(q, q)
            silu_of(0, 0)
            silu_of(1, 1)
            for p in range(PLACES):
                expert_step(p, p)
            with act.Fori(1, PAIRS // PLACES - 1) as g:
                for k in range(PLACES):
                    expert_step(g * PLACES + k, k)
            for k in range(PLACES):
                expert_step(PAIRS - PLACES + k, k)
            y_store(PAIRS - 1, PLACES - 1)

            def shared_gate(i):
                act.wait_ge(s1_full, i + 1)
                wait(act, shared_hidden_ready, i)
                act.activation(shared_silu[:].rearrange("p c d -> p (c d)"), banks[0][:], ACT.Silu).then_inc(shared_silu_ready, 1)

            shared_gate(0)
            with act.Fori(1, NB) as i:
                shared_gate(i)

        @block.vector
        def _(dve):
            dve.wait_ge(w_ids, 16)
            dve.tensor_scalar(not_pad[:], ids_sb[:], float(PADDING_IDX), None, ALU.not_equal).then_inc(pad_made, 1)
            dve.sem_inc(seen_made, 1)

            def mean_var(stats, mv, var, source, s_stats, s_mean, s_var, n):
                carried(dve)
                for c in range(C):
                    dve.bn_stats(stats[:, c, :], source[:, c, :]).then_inc(s_stats, 1)
                dve.wait_ge(s_stats, n * C)
                carried(dve)
                for c in range(C):
                    dve.bn_aggr(mv[:, c, :], stats[:, c, :]).then_inc(s_mean, 1)
                dve.wait_ge(s_mean, n * C)
                dve.tensor_scalar(var[:], mv[:, :, 1], LN_EPS, None, ALU.add).then_inc(s_var, 1)

            def shift(out_ap, mv, rstd, rstd_ready, ready, n):
                dve.wait_ge(rstd_ready, n)
                dve.scalar_tensor_tensor(out_ap[:], mv[:, :, 0], -1.0, rstd[:], ALU.mult, ALU.mult).then_inc(ready, 1)

            def ln_first(i):
                dve.wait_ge(emb_masked, i * C + C)
                mean_var(stats1, mv1, var1, emb, ln1_stats, ln1_mean, ln1_var, i + 1)

            def rest(i, name, hi, lo, scale=1.0):
                b = banks[front_bank(name)]
                count = front_count(i, name)
                after_x = FRONT.index(name) > FRONT.index("X")
                if name == "T1":
                    count = count - i if isinstance(i, int) else (i - 1) * (NF - 1) + (FRONT.index("T1") + 1)
                else:
                    count = i * (NF - 1) + (count - i * NF if isinstance(i, int) else FRONT.index(name) + 2) - after_x
                dve.wait_ge(front_hi, count)
                src = b[:] if len(hi.shape) == 2 else b[:].rearrange("p (a b) -> p a b", b=P)
                dve.scalar_tensor_tensor(lo, src, scale, hi.bitcast(F32), ALU.mult, ALU.subtract).then_inc(front_free, 1)

            def states(i):
                b = banks[front_bank("X")]
                dve.wait_ge(front_full, front_count(i, "X"))
                wait(dve, state_split, i)
                dve.tensor_copy(state[:, 0, :], b[:, 0:D]).then_inc(state_step, 1)
                dve.wait_ge(state_step, i * 3 + 1)
                dve.tensor_tensor(state[:, 1, :], state[:, 0, :], b[:, D:2 * D], ALU.add).then_inc(state_step, 1)
                dve.wait_ge(state_step, i * 3 + 2)
                dve.tensor_tensor(state[:, 2, :], state[:, 1, :], b[:, 2 * D:3 * D], ALU.add).then_inc(state_step, 1)
                dve.wait_ge(state_step, i * 3 + 3)
                dve.sem_inc(front_free, 1)

            def residual(n):
                dve.wait_ge(full["Y"], n)
                dve.wait_ge(xt_ready, n)
                dve.tensor_tensor(vt[:], banks[back_bank("Y")][:], xt[:], ALU.add).then_inc(free["Y"], 1)

            def ln_mid(n):
                dve.wait_ge(full["T2"], n)
                v = banks[back_bank("T2")][:].rearrange("p (c d) -> p c d", d=D)
                mean_var(stats2, mv2, var2, v, ln2_stats, ln2_mean, ln2_var, n)

            def m1_low(n, j):
                dve.wait_ge(free["W1a" if j == 0 else "W1b"], n)
                dve.tensor_tensor(m1_lo[:, j], m1[:, j], m1_hi[:, j].bitcast(F32), ALU.subtract).then_inc(m1_split, 1)

            def mlp_out(n):
                dve.wait_ge(full["W2"], n)
                dve.scalar_tensor_tensor(z2t[:], banks[back_bank("W2")][:], b2_sb[:], zt[:], ALU.add, ALU.add).then_inc(free["W2"], 1)

            def attn_out(n, i):
                dve.wait_ge(full["WP"], n)
                dve.wait_ge(stream_begun, n)
                h = stream[:, tile_slice(i), :]
                dve.tensor_tensor(h, banks[back_bank("WP")][:].rearrange("p (c d) -> p c d", d=D), h, ALU.add).then_inc(free["WP"], 1)

            def ln_last(n, i):
                dve.wait_ge(free["WP"], n)
                carried(dve)
                for c in range(C):
                    dve.bn_stats(stats3[:, c, :], stream[:, bass.ds(i * C + c, 1), :].rearrange("p a d -> p (a d)")).then_inc(ln3_stats, 1)
                dve.wait_ge(ln3_stats, n * C)
                carried(dve)
                for c in range(C):
                    dve.bn_aggr(mv3[:, c, :], stats3[:, c, :]).then_inc(ln3_mean, 1)
                dve.wait_ge(ln3_mean, n * C)
                dve.tensor_scalar(var3[:], mv3[:, :, 1], LN_EPS, None, ALU.add).then_inc(ln3_var, 1)

            def choose(n, half=None):
                t = tiles_of(half)
                at = slice(t[0], t[-1] + 1)
                dve.wait_ge(free["G"], upto(n, half))
                carried(dve)
                for c in t:
                    dve.max(top8[:, c, :], scores[:, c, :]).then_inc(top_found, 1)
                dve.wait_ge(top_found, tiles_upto(n, half))
                carried(dve)
                for c in t:
                    dve.max_index(index8[:, c, :], top8[:, c, :], scores[:, c, :]).then_inc(index_found, 1)
                dve.wait_ge(index_found, tiles_upto(n, half))
                dve.tensor_copy(index2[:, :, at], index8[:, at, 0:TOP_K].rearrange("p c k -> p k c")).then_inc(index_float, 1)

            def choose_either(n, half=None):
                t = tiles_of(half)
                at, shape = slice(t[0], t[-1] + 1), [P, TOP_K, len(t), E]
                dve.wait_ge(index_float, upto(n, half))
                dve.tensor_tensor(chosen[:, :, at], index2[:, :, at].unsqueeze(3).broadcast_to(shape),
                                  expert_iota[:].unsqueeze(1).unsqueeze(1).broadcast_to(shape),
                                  ALU.is_equal).then_inc(chosen_made, 1)
                dve.wait_ge(chosen_made, upto(n, half))
                dve.tensor_tensor(either[:, at], chosen[:, 0, at], chosen[:, 1, at], ALU.add).then_inc(either_made, 1)
                dve.wait_ge(either_made, upto(n, half))

            def route(n, half=None):
                t = tiles_of(half)
                at = slice(t[0], t[-1] + 1)
                dve.wait_ge(full["C"], upto(n, half))
                before = back_place("C", half)[:, t[0] * E:(t[-1] + 1) * E].rearrange("p (c e) -> p c e", e=E)
                for k in range(TOP_K):
                    op = dve.tensor_tensor(chosen_pos[:, k, at], before, chosen[:, k, at], ALU.mult)
                    op.then_inc(pos_made, 1)
                dve.sem_inc(free["C"], 1)
                if half is None:
                    dve.tensor_reduce(seen_new[:], either[:].rearrange("p c e -> p e c"), AXES.X, ALU.add).then_inc(seen_sum, 1)
                dve.wait_ge(pos_made, upto(n, half) * 3 - 1)
                dve.tensor_reduce(pos[:, :, at], chosen_pos[:, :, at], AXES.X, ALU.add).then_inc(pos_made, 1)
                if half is None:
                    dve.wait_ge(seen_sum, n)
                    dve.tensor_tensor(seen[:], seen[:], seen_new[:], ALU.add).then_inc(seen_made, 1)

            def slots(n, i, half=None):
                t = tiles_of(half)
                at = slice(t[0], t[-1] + 1)
                m = upto(n, half)
                dve.wait_ge(pos_made, m * 3)
                dve.tensor_scalar(kept[:, :, at], pos[:, :, at], float(CAP), None, ALU.is_lt).then_inc(kept_made, 1)
                dve.tensor_scalar(pos_in[:, :, at], pos[:, :, at], float(CAP - 1), None, ALU.min).then_inc(kept_made, 1)
                dve.wait_ge(kept_made, m * 2)
                dve.scalar_tensor_tensor(slot_f[:, :, at], index2[:, :, at], float(CAP), pos_in[:, :, at],
                                         ALU.mult, ALU.add).then_inc(slot_made, 1)
                dve.tensor_scalar(slot_drop[:, :, at], kept[:, :, at], -float(DROPPED), float(DROPPED),
                                  ALU.mult, ALU.add).then_inc(slot_made, 1)
                wait(dve, rows_sent, (n - 1) * (16 * TOP_K * C))
                dve.wait_ge(slot_made, m * 2)
                dve.tensor_tensor(slot_out[:].rearrange("p (k c) -> p k c", c=C)[:, :, at], slot_f[:, :, at],
                                  slot_drop[:, :, at], ALU.add).then_inc(slots_ready, 1)
                if half != 0:
                    dve.tensor_copy(pair_slot[:, bass.ds(i, 1), :].rearrange("p b (k c) -> p (b k) c", c=C),
                                    slot_f[:]).then_inc(slots_kept, 1)

            def weights(n, i):
                tops = top8[:, :, 0:TOP_K].rearrange("p c k -> p k c")
                dve.tensor_tensor(top_sum[:], tops[:, 0], tops[:, 1], ALU.add).then_inc(weight_step, 1)
                dve.wait_ge(weight_step, n * 4 - 3)
                dve.tensor_scalar(top_sum[:], top_sum[:], 1e-20, None, ALU.add).then_inc(weight_step, 1)
                dve.wait_ge(weight_step, n * 4 - 2)
                dve.reciprocal(top_inv[:], top_sum[:]).then_inc(weight_step, 1)
                dve.wait_ge(weight_step, n * 4 - 1)
                dve.tensor_tensor(weight[:], tops, top_inv[:].unsqueeze(1).broadcast_to([P, TOP_K, C]), ALU.mult).then_inc(weight_step, 1)
                dve.wait_ge(weight_step, n * 4)
                dve.scalar_tensor_tensor(pair_weight[:, bass.ds(i, 1), :].rearrange("p b (k c) -> p (b k) c", c=C),
                                         weight[:], ROUTE_SCALE, kept[:], ALU.mult, ALU.mult).then_inc(weight_ready, 1)

            def weights_low():
                dve.wait_ge(p_hi_made, 1)
                dve.tensor_tensor(p_lo[:], raw_p[:], p_hi[:].bitcast(F32), ALU.subtract).then_inc(p_lo_made, 1)
                dve.wait_ge(mlp_hi_made, 2)
                dve.tensor_tensor(w1_lo[:], w1_sb[:], w1_hi[:].bitcast(F32), ALU.subtract).then_inc(mlp_lo_made, 1)
                dve.tensor_tensor(w2_lo[:], w2_sb[:], w2_hi[:].bitcast(F32), ALU.subtract).then_inc(mlp_lo_made, 1)

            def batch(i, more, behind, routed):
                for name in FRONT:
                    k = int(name[-1]) if name != "X" else 0
                    if name.startswith("Q"):
                        rest(i, name, qz_hi[:, k, :], qz_lo[:, k, :], SCORE_SCALE)
                    elif name == "X":
                        states(i)
                    elif name.startswith("SC"):
                        rest(i, name, sc_hi[:, k % 4], sc_lo[:, k % 4])
                    elif name.startswith("U"):
                        c, g = k // 2, k % 2
                        at = (slice(None), slice(HG * g, HG * g + HG), slice(c * P, (c + 1) * P))
                        rest(i, name, ut_hi[at], ut_lo[at])
                    elif name == "T1" and more:
                        rest(i + 1, "T1", xt_hi[:], xt_lo[:])
                    if name == "Q3" and behind:
                        ln_mid(i)
                    if name == "Q6" and behind:
                        shift(shift2, mv2, rstd2, ln2_rstd, ln2_shift, i)
                    if name == "SC1" and routed:
                        choose(i - 1)
                    if name == "SC3" and routed:
                        choose_either(i - 1)
                    if name == "SC4" and more:
                        ln_first(i + 1)
                    if name == "U1" and behind:
                        m1_low(i, 0)
                    if name == "SC5":
                        if more:
                            shift(shift1, mv1, rstd1, ln1_rstd, ln1_shift, i + 2)
                        if behind:
                            m1_low(i, 1)
                    if name == "U3" and routed:
                        route(i - 1)
                    if name == "SC7" and behind:
                        mlp_out(i)
                    if name == "U4" and not behind:
                        weights_low()
                    if name == "U5" and routed:
                        slots(i - 1, i - 2)
                    if name == "T1" and behind:
                        attn_out(i, i - 1)
                    if name == "U7":
                        if behind:
                            ln_last(i, i - 1)
                        if routed:
                            weights(i - 1, i - 2)
                        if behind:
                            shift(shift3, mv3, rstd3, ln3_rstd, ln3_shift, i)
                        residual(i + 1)

            dve.wait_ge(q_hi_made, 1)
            dve.tensor_tensor(q_lo[:], raw_q[:], q_hi[:].bitcast(F32), ALU.subtract).then_inc(q_lo_made, 1)
            ln_first(0)
            shift(shift1, mv1, rstd1, ln1_rstd, ln1_shift, 1)
            rest(0, "T1", xt_hi[:], xt_lo[:])
            batch(0, True, False, False)
            dve.wait_ge(const_made, 6)
            batch(1, True, True, False)
            batch(2, True, True, True)
            with dve.Fori(3, NB - 1) as i:
                batch(i, True, True, True)
            batch(NB - 1, False, True, True)
            ln_mid(NB)
            choose(NB - 1)
            shift(shift2, mv2, rstd2, ln2_rstd, ln2_shift, NB)
            choose_either(NB - 1)
            route(NB - 1)
            m1_low(NB, 0)
            m1_low(NB, 1)
            slots(NB - 1, NB - 2)
            mlp_out(NB)
            weights(NB - 1, NB - 2)
            attn_out(NB, NB - 1)
            ln_last(NB, NB - 1)
            shift(shift3, mv3, rstd3, ln3_rstd, ln3_shift, NB)
            choose(NB, 0)
            choose_either(NB, 0)
            route(NB, 0)
            slots(NB, NB - 1, 0)
            choose(NB, 1)
            choose_either(NB, 1)
            route(NB, 1)
            slots(NB, NB - 1, 1)
            weights(NB, NB - 1)

            def w13_high(q, k):
                wait(dve, gu_full, q - (PLACES - 1))
                dve.tensor_copy(w13_hi[k][:], w13_all[:, bass.ds(q, 1)].rearrange("p q e f -> p (q e) f")).then_inc(w13_hi_ready, 1)

            def rows_out(q, k):
                dve.wait_ge(rows_t_hi_ready, q + 1)
                dve.tensor_tensor(rows_t_lo[k], banks[k % 2][:], rows_t_hi[k].bitcast(F32), ALU.subtract).then_inc(rows_t_ready, 1)

            def hidden_of(q, k):
                dve.wait_ge(silu_ready, q + 1)
                wait(dve, y_full, q - 1)
                dve.tensor_tensor(hidden[k % 2][0:EH, :], banks[2 + k][EH:P, :], silu[k % 2][EH:P, :], ALU.mult).then_inc(hidden_ready, 1)

            def expert_step(p, k):
                if not (isinstance(p, int) and p + 4 >= PAIRS):
                    rows_out(p + 4, k)
                if not (isinstance(p, int) and p + 2 >= PAIRS):
                    hidden_of(p + 2, (k + 2) % PLACES)
                if not (isinstance(p, int) and p + PLACES >= PAIRS):
                    w13_high(p + PLACES, k)

            dve.wait_ge(expert_weights, 16 * 2)
            for k in range(PLACES):
                w13_high(k, k)
            for q in range(PLACES):
                rows_out(q, q)
            hidden_of(0, 0)
            hidden_of(1, 1)
            for p in range(PLACES):
                expert_step(p, p)
            with dve.Fori(1, PAIRS // PLACES - 1) as g:
                for k in range(PLACES):
                    expert_step(g * PLACES + k, k)
            for k in range(PLACES):
                expert_step(PAIRS - PLACES + k, k)

            def shared(i):
                dve.wait_ge(shared_silu_ready, i + 1)
                dve.wait_ge(s3_full, i + 1)
                dve.tensor_tensor(shared_hidden[:].rearrange("p c d -> p (c d)"), banks[1][:],
                                  shared_silu[:].rearrange("p c d -> p (c d)"), ALU.mult).then_inc(shared_hidden_ready, 1)
                dve.wait_ge(s2_full, i + 1)
                h = stream[:, tile_slice(i), :]
                dve.tensor_tensor(h, banks[2][:].rearrange("p (c d) -> p c d", d=D), h, ALU.add).then_inc(shared_added, 1)

            def add_pairs(i, k, landed):
                dve.wait_ge(shared_added, i + 1)
                for m in range(TOP_K * C):
                    dve.wait_ge(y_landed[k][m], landed)
                    if m == C:
                        dve.wait_ge(pair_added, i * C + C)
                    h = stream[:, bass.ds(i * C + m % C, 1), :].rearrange("p a d -> p (a d)")
                    w = pair_weight[:, bass.ds(i, 1), m:m + 1].rearrange("p a m -> p (a m)")
                    op = dve.scalar_tensor_tensor(h, y_got[k][:, m, :], w, h, ALU.mult, ALU.add)
                    if m < C:
                        op.then_inc(pair_added, 1)
                op.then_inc(tiles_done, 1)

            dve.wait_ge(weight_ready, NB)
            with dve.Fori(0, NB // 2) as g:
                for k in range(2):
                    shared(g * 2 + k)
                    add_pairs(g * 2 + k, k, g * 16 + 16)

        @block.tensor
        def _(pe):
            def product(out_ap, pairs, start=True, stop=True):
                last = None
                for n, (ah, al, bh, bl) in enumerate(pairs):
                    pe.matmul(out_ap, ah, bh, start=start and n == 0, stop=False)
                    pe.matmul(out_ap, ah, bl, start=False, stop=False)
                    last = pe.matmul(out_ap, al, bh, start=False, stop=stop and n == len(pairs) - 1)
                return last

            def front_slot(i, name):
                wait(pe, front_free, front_before(i, name))
                return banks[front_bank(name)]

            def back_slot(n, name):
                _, before, further = BACK[name]
                if n is NB and name in LAST_BEFORE:
                    before, further = LAST_BEFORE[name]
                wait(pe, free[before], n + further)
                return banks[back_bank(name)]

            def transposes(dst, src, tiles=range(C)):
                for c in tiles:
                    op = pe.transpose(dst[:, c * P:(c + 1) * P], src(c), identity[:])
                return op

            def t1(i):
                b = front_slot(i, "T1")
                for c in range(C):
                    pe.wait_ge(xn_ready, i * C + c + 1)
                    op = transposes(b, lambda c: xn[:, c, :], [c])
                op.then_inc(front_full, 1)

            def qz(i, h):
                b = front_slot(i, f"Q{h}")
                product(b[:], [(q_hi[:, h, :], q_lo[:, h, :], xt_hi[:], xt_lo[:])]).then_inc(front_full, 1)

            def outer(i):
                b = front_slot(i, "X")
                pe.wait_ge(x_split, i + 1)
                for c in range(C - 1):
                    op = product(b[:, c * D:(c + 1) * D], [(x_hi[:, c, :], x_lo[:, c, :], x_hi[:, c, :], x_lo[:, c, :])])
                op.then_inc(front_full, 1)

            def score(i, k):
                c, g = k // 2, k % 2
                b = front_slot(i, f"SC{k}")
                at = (slice(None), slice(HG * g, HG * g + HG), slice(c * P, (c + 1) * P))
                xs = slice(c * P, (c + 1) * P)
                product(b[:].rearrange("p (a b) -> p a b", b=P),
                        [(xt_hi[:, xs], xt_lo[:, xs], qz_hi[at], qz_lo[at])]).then_inc(front_full, 1)

            def weighted(i, k):
                c, g = k // 2, k % 2
                b = front_slot(i, f"U{k}")
                at = (slice(None), slice(HG * g, HG * g + HG), slice(c * P, (c + 1) * P))
                pe.wait_ge(masked, i * GROUPS + k + 1)
                pairs = [(x_hi[:, c, :], x_lo[:, c, :], sc_hi[:, k % 4], sc_lo[:, k % 4])]
                if c:
                    if k == 2:
                        pe.wait_ge(state_split, i + 1)
                    pairs.append((st_hi[:, c - 1, :], st_lo[:, c - 1, :], qz_hi[at], qz_lo[at]))
                product(b[:].rearrange("p (a b) -> p a b", b=P), pairs).then_inc(front_full, 1)

            def y_product(n):
                b = back_slot(n, "Y")
                pe.wait_ge(p_lo_made, 1)
                for g in range(2):
                    pe.wait_ge(front_free, front_count(n - 1, f"U{GROUPS - 2 + g}"))
                    op = product(b[:], [(p_hi[:, h, :], p_lo[:, h, :], ut_hi[:, h, :], ut_lo[:, h, :]) for h in range(HG * g, HG * g + HG)],
                                 start=g == 0, stop=g == 1)
                op.then_inc(full["Y"], 1)

            def t2(n):
                b = back_slot(n, "T2")
                pe.wait_ge(free["Y"], n)
                transposes(b, lambda c: vt[:, c * P:(c + 1) * P]).then_inc(full["T2"], 1)

            def t3(n):
                b = back_slot(n, "T3")
                pe.wait_ge(free["T2"], n)
                transposes(b, lambda c: z0[:, c, :]).then_inc(full["T3"], 1)

            def mlp_in(n):
                pe.wait_ge(zt_split, n)
                for j, name in enumerate(("W1a", "W1b")):
                    b = back_slot(n, name)
                    at = slice(j * P, (j + 1) * P)
                    product(b[:], [(w1_hi[:, at], w1_lo[:, at], zt_hi[:], zt_lo[:])]).then_inc(full[name], 1)

            def mlp_down(n):
                b = back_slot(n, "W2")
                pe.wait_ge(m1_split, n * 2)
                product(b[:], [(w2_hi[:, j], w2_lo[:, j], m1_hi[:, j], m1_lo[:, j]) for j in range(2)]).then_inc(full["W2"], 1)

            def project(n):
                b = back_slot(n, "WP")
                pe.wait_ge(free["W2"], n)
                for c in range(C):
                    op = pe.matmul(b[:, c * D:(c + 1) * D], z2t[:, c * P:(c + 1) * P], wp_sb[:], start=True, stop=True)
                op.then_inc(full["WP"], 1)

            def t4(n, half=None):
                back_slot(n, "T4")
                b = back_place("T4", half)
                pe.wait_ge(xf_ready, upto(n, half))
                transposes(b, lambda c: xf[:, c, :], tiles_of(half)).then_inc(full["T4"], 1)

            def gate(n, half=None):
                back_slot(n, "G")
                b = back_place("G", half)
                pe.wait_ge(xft_ready, upto(n, half))
                for c in tiles_of(half):
                    op = pe.matmul(b[:, c * E:(c + 1) * E], xft[:, c * P:(c + 1) * P], gate_sb[:], start=True, stop=True)
                op.then_inc(full["G"], 1)

            def counts(n, half=None):
                t = tiles_of(half)
                at = slice(t[0] * E, (t[-1] + 1) * E)
                back_slot(n, "C")
                b = back_place("C", half)
                pe.wait_ge(either_made, upto(n, half))
                pe.wait_ge(seen_made, n)
                pe.matmul(b[:, at], upper[:], either[:, t[0]:t[-1] + 1], start=True, stop=False)
                for c in t:
                    for before in range(c):
                        pe.matmul(b[:, c * E:(c + 1) * E], ones[:], either[:, before, :], start=False, stop=False)
                op = pe.matmul(b[:, at], ones[:], seen[:].unsqueeze(1).broadcast_to([P, len(t), E]), start=False, stop=True)
                op.then_inc(full["C"], 1)

            def batch(i, more, behind, routed):
                pe.wait_ge(front_free, front_count(i, "T1"))
                for name in FRONT:
                    k = int(name[-1]) if name != "X" else 0
                    if name.startswith("Q"):
                        if front_bank(name) == front_bank("T1"):
                            pe.wait_ge(xt_ready, i + 1)
                        qz(i, k)
                    elif name == "X":
                        outer(i)
                    elif name.startswith("SC"):
                        if k < 2:
                            pe.wait_ge(front_free, front_count(i, f"Q{HG * k + HG - 1}"))
                        score(i, k)
                    elif name.startswith("U"):
                        weighted(i, k)
                    elif name == "T1" and more:
                        t1(i + 1)
                    if name == "Q1" and routed:
                        t4(i - 1)
                    if name == "Q4" and behind:
                        t2(i)
                    if name == "Q6" and routed:
                        gate(i - 1)
                    if name == "SC2" and behind:
                        t3(i)
                    if name == "SC5" and behind:
                        mlp_in(i)
                    if name == "SC6" and routed:
                        counts(i - 1)
                    if name == "U5" and behind:
                        mlp_down(i)
                    if name == "U7" and behind:
                        project(i)
                y_product(i + 1)

            pe.wait_ge(const_made, 6)
            t1(0)
            pe.wait_ge(q_lo_made, 1)
            batch(0, True, False, False)
            pe.wait_ge(w_small, 16 * SMALL)
            pe.wait_ge(mlp_lo_made, 2)
            batch(1, True, True, False)
            batch(2, True, True, True)
            with pe.Fori(3, NB - 1) as i:
                batch(i, True, True, True)
            batch(NB - 1, False, True, True)
            t4(NB - 1)
            t2(NB)
            gate(NB - 1)
            t3(NB)
            counts(NB - 1)
            mlp_in(NB)
            mlp_down(NB)
            project(NB)
            t4(NB, 0)
            t4(NB, 1)
            gate(NB, 0)
            gate(NB, 1)
            counts(NB, 0)
            counts(NB, 1)

            def rows_in(q, k):
                pe.wait_ge(rows_landed[k], q * (16 // PLACES) - k * (16 // PLACES) + 16)
                wait(pe, rows_t_ready, q - 1)
                for m in range(4):
                    op = pe.transpose(banks[k % 2][:, m * P:(m + 1) * P],
                                      rows[k][:, m // 2, (m % 2) * D:(m % 2 + 1) * D], identity[:])
                op.then_inc(rows_t_full, 1)

            def gate_up(q, k):
                pe.wait_ge(rows_t_ready, q + 1)
                pe.wait_ge(w13_split, q + 1)
                wait(pe, hidden_ready, q - (PLACES - 1))
                for e in range(2):
                    at = slice(e * 2 * P, (e + 1) * 2 * P)
                    op = product(banks[2 + k][:, at], [(w13_hi[k][:, e, :], w13_lo[k][:, e, :], rows_t_hi[k][:, at], rows_t_lo[k][:, at])])
                op.then_inc(gu_full, 1)

            def down(q, k):
                pe.wait_ge(hidden_ready, q + 1)
                wait(pe, y_ready, q - 1)
                for m in range(4):
                    op = pe.matmul(banks[6 + k % 2][:, m * D:(m + 1) * D], hidden[k % 2][0:EH, m * P:(m + 1) * P],
                                   w2_all[0:EH, bass.ds(q, 1), m // 2, :].rearrange("p q d -> p (q d)"),
                                   start=True, stop=True)
                op.then_inc(y_full, 1)

            def expert_step(p, k):
                if not (isinstance(p, int) and p + 4 >= PAIRS):
                    rows_in(p + 4, k)
                if not (isinstance(p, int) and p + 2 >= PAIRS):
                    gate_up(p + 2, (k + 2) % PLACES)
                down(p, k)

            pe.wait_ge(expert_weights, 16 * 2)
            pe.wait_ge(free["T4"], NB + 1)
            pe.wait_ge(free["C"], NB + 1)
            for q in range(PLACES):
                rows_in(q, q)
            gate_up(0, 0)
            gate_up(1, 1)
            for p in range(PLACES):
                expert_step(p, p)
            with pe.Fori(1, PAIRS // PLACES - 1) as g:
                for k in range(PLACES):
                    expert_step(g * PLACES + k, k)
            for k in range(PLACES):
                expert_step(PAIRS - PLACES + k, k)

            pe.wait_ge(hidden_ready, PAIRS)
            def shared(i):
                x = xft_all[:, bass.ds(i, 1), :].rearrange("p b s -> p (b s)")
                wait(pe, shared_silu_ready, i)
                pe.matmul(banks[0][:], sw1_sb[:], x, start=True, stop=True).then_inc(s1_full, 1)
                wait(pe, shared_hidden_ready, i)
                pe.matmul(banks[1][:], sw3_sb[:], x, start=True, stop=True).then_inc(s3_full, 1)
                pe.wait_ge(shared_hidden_ready, i + 1)
                wait(pe, shared_added, i)
                for c in range(C):
                    op = pe.matmul(banks[2][:, c * D:(c + 1) * D], shared_hidden[:, c, :], sw2_sb[:], start=True, stop=True)
                op.then_inc(s2_full, 1)

            shared(0)
            with pe.Fori(1, NB) as i:
                shared(i)


def kernel(**inputs):
    import numpy as np
    import concourse.bacc as bacc
    from concourse.bass_utils import run_bass_kernel_spmd

    a = {k: np.asarray(v) for k, v in inputs.items()}
    nb, s = a["x"].shape
    d = a["L0_tok_W"].shape[0]
    e, _, eh = a["L0_ffn_w1"].shape
    tiles = nb * s // P
    w13 = np.concatenate([a["L0_ffn_w1"], a["L0_ffn_w3"]], axis=2)
    laid = {
        "ids": a["x"].reshape(tiles, P).T,
        "embed": a["L0_tok_W"].T,
        "pT": a["L0_attn_P"].transpose(2, 0, 1),
        "qT": a["L0_attn_Q"].transpose(2, 0, 1),
        "gamma": a["L0_attn_gamma"].reshape(d, 1),
        "beta": a["L0_attn_beta"].reshape(d, 1),
        "w1T": a["L0_attn_W1"].T,
        "b1": a["L0_attn_b1"].reshape(2, d).T,
        "w2T": a["L0_attn_W2"].T.reshape(2, d, d).transpose(1, 0, 2),
        "b2": a["L0_attn_b2"].reshape(d, 1),
        "wpT": a["L0_attn_Wp"].T,
        "bp": a["L0_attn_bp"].reshape(1, d),
        "gateT": a["L0_ffn_gate_w"].T,
        "ew13": w13.reshape(e // 2, 2, d, 2 * eh).transpose(0, 2, 1, 3),
        "ew2": a["L0_ffn_w2"].reshape(e // 2, 2, eh, d).transpose(0, 2, 1, 3),
        "sw1": a["L0_ffn_sw1"],
        "sw3": a["L0_ffn_sw3"],
        "sw2": a["L0_ffn_sw2"],
    }
    nc = bacc.Bacc("TRN2", target_bir_lowering=False, num_devices=1)
    arrays, args = {}, []
    for name, v in laid.items():
        v = np.ascontiguousarray(v)
        arrays[f"in_{name}"] = v
        args.append(nc.dram_tensor(f"in_{name}", v.shape, mybir.dt.from_np(v.dtype), kind="ExternalInput").ap())
    args.append(nc.dram_tensor("out_0", (nb, s, d), F32, kind="ExternalOutput").ap())
    tower(nc, *args)
    r = run_bass_kernel_spmd(nc, [arrays], core_ids=[0])
    return r.results[0]["out_0"]
```
